# Optimizing a Trainium2 kernel written in Bass

```python
import numpy as np
import jax
import jax.numpy as jnp

def _softmax(x, axis=-1):
    return jax.nn.softmax(x, axis=axis)

def _gelu(x):
    return jax.nn.gelu(x, approximate=True)

def _silu(x):
    return jax.nn.silu(x)

def _sigmoid(x):
    return jax.nn.sigmoid(x)

def _layernorm(x, axis=-1, eps=1e-05):
    m = jnp.mean(x, axis=axis, keepdims=True)
    v = jnp.var(x, axis=axis, keepdims=True)
    return (x - m) / jnp.sqrt(v + eps)

def _scatter_add(tgt, idx, src, axis=0):
    return tgt.at[idx].add(src)

def _segment_sum(src, seg, n):
    return jax.ops.segment_sum(src, seg, n)
kernel_name = 'mk_adj_ffn_d1_adj_r2_9a0968'

def setup_inputs(seed: int=0):
    np.random.seed(seed)
    _w = jnp.asarray

    def _rec_inputs():
        import jax
        import jax.numpy as jnp
        _gk = jax.random.key(seed)
        x = -0.001547 + 1.001 * jax.random.normal(jax.random.fold_in(_gk, 1), (512, 128), jnp.float32)
        _w = (1.0 + jnp.arange(512, dtype=jnp.float32)) ** (-0.5)
        _w = _w / _w.mean()
        _pij = jnp.clip(0.03125 * _w[:, None] * _w[None, :], 0.0, 1.0)
        _a = jax.random.uniform(jax.random.fold_in(_gk, 2), (512, 512)) < _pij
        adj = _a.astype(jnp.int32)
        return (x, adj)
    x, adj = _rec_inputs()

    def _L0_gnn_setup():
        import jax, jax.numpy as jnp
        import numpy as np
        BT, BN, D, H = (512, 512, 128, 8)
        DH = D // H
        key = jax.random.key(seed)
        ks = jax.random.split(key, 16)
        s = 1.0 / np.sqrt(D)
        return {'h_target': jax.random.normal(ks[0], (BT, D), jnp.float32), 'h_neigh': jax.random.normal(ks[1], (BN, D), jnp.float32), 'adjacency': jax.random.randint(ks[2], (BT, BN), 0, 2, jnp.int32), 'edge_types': jax.random.randint(ks[3], (BT, BN), 0, 2, jnp.int32), 'Wq': jax.random.normal(ks[4], (D, D), jnp.float32) * s, 'bq': jnp.zeros((D,), jnp.float32), 'Wk': jax.random.normal(ks[5], (D, D), jnp.float32) * s, 'bk': jnp.zeros((D,), jnp.float32), 'Wv': jax.random.normal(ks[6], (D, D), jnp.float32) * s, 'bv': jnp.zeros((D,), jnp.float32), 'Wo': jax.random.normal(ks[7], (D, D), jnp.float32) * s, 'bo': jnp.zeros((D,), jnp.float32), 'E': jax.random.normal(ks[8], (2, D), jnp.float32)}
    _L0_gnn_all = _L0_gnn_setup()
    _L0_gnn_in = {k: v for k, v in _L0_gnn_all.items() if k in ('h_neigh', 'Wq', 'bq', 'Wk', 'bk', 'Wv', 'bv', 'Wo', 'bo', 'E')}
    del _L0_gnn_all

    def _L0_ffn_setup():
        import jax, jax.numpy as jnp
        import numpy as np
        INPUT_WIDTH = 128
        DEPTH = 7
        OUTPUT_WIDTH = 128
        N_NODES = 2 ** (DEPTH + 1) - 1
        key = jax.random.key(seed)
        k_x, k_w1, k_w2 = jax.random.split(key, 3)
        init1 = 1.0 / np.sqrt(INPUT_WIDTH)
        x = jax.random.normal(k_x, (2, 512, INPUT_WIDTH), dtype=jnp.float32)
        w1s = jax.random.uniform(k_w1, (N_NODES, INPUT_WIDTH), jnp.float32, -init1, init1)
        b1s = jnp.zeros((N_NODES,), jnp.float32)
        w2s = jax.random.uniform(k_w2, (N_NODES, INPUT_WIDTH, OUTPUT_WIDTH), jnp.float32, -init1, init1)
        b2s = jnp.zeros((N_NODES, OUTPUT_WIDTH), jnp.float32)
        return {'x': x, 'w1s': w1s, 'b1s': b1s, 'w2s': w2s, 'b2s': b2s}
    _L0_ffn_all = _L0_ffn_setup()
    _L0_ffn_in = {k: v for k, v in _L0_ffn_all.items() if k in ('w1s', 'b1s', 'w2s', 'b2s')}
    del _L0_ffn_all
    return {'x': x, 'adj': adj, 'L0_gnn_h_neigh': _L0_gnn_in['h_neigh'], 'L0_gnn_Wq': _L0_gnn_in['Wq'], 'L0_gnn_bq': _L0_gnn_in['bq'], 'L0_gnn_Wk': _L0_gnn_in['Wk'], 'L0_gnn_bk': _L0_gnn_in['bk'], 'L0_gnn_Wv': _L0_gnn_in['Wv'], 'L0_gnn_bv': _L0_gnn_in['bv'], 'L0_gnn_Wo': _L0_gnn_in['Wo'], 'L0_gnn_bo': _L0_gnn_in['bo'], 'L0_gnn_E': _L0_gnn_in['E'], 'L0_ffn_w1s': _L0_ffn_in['w1s'], 'L0_ffn_b1s': _L0_ffn_in['b1s'], 'L0_ffn_w2s': _L0_ffn_in['w2s'], 'L0_ffn_b2s': _L0_ffn_in['b2s']}

def reference(x, adj, L0_gnn_h_neigh, L0_gnn_Wq, L0_gnn_bq, L0_gnn_Wk, L0_gnn_bk, L0_gnn_Wv, L0_gnn_bv, L0_gnn_Wo, L0_gnn_bo, L0_gnn_E, L0_ffn_w1s, L0_ffn_b1s, L0_ffn_w2s, L0_ffn_b2s):
    import jax
    import jax.numpy as jnp

    def _L0_gnn_ref(h_target, h_neigh, adjacency, edge_types, Wq, bq, Wk, bk, Wv, bv, Wo, bo, E):
        import jax, jax.numpy as jnp
        import numpy as np
        BT, BN, D, H = (512, 512, 128, 8)
        DH = D // H
        Bt, d = h_target.shape
        Bn = h_neigh.shape[0]
        msg = h_neigh[None, :, :] + E[edge_types]
        q = (h_target @ Wq.T + bq).reshape(Bt, H, DH)
        k = (msg @ Wk.T + bk).reshape(Bt, Bn, H, DH)
        v = (msg @ Wv.T + bv).reshape(Bt, Bn, H, DH)
        scores = jnp.einsum('bhd,bnhd->bhn', q, k) / np.sqrt(DH).astype(np.float32)
        mask = adjacency[:, None, :] == 0
        scores = jnp.where(mask, jnp.float32(-1000000000.0), scores)
        attn = jax.nn.softmax(scores, axis=-1)
        attn = jnp.where(mask, jnp.float32(0.0), attn)
        out = jnp.einsum('bhn,bnhd->bhd', attn, v).reshape(Bt, d)
        return out @ Wo.T + bo

    def _L0_ffn_ref(x, w1s, b1s, w2s, b2s):
        import jax, jax.numpy as jnp
        import numpy as np
        INPUT_WIDTH = 128
        DEPTH = 7
        OUTPUT_WIDTH = 128
        N_NODES = 2 ** (DEPTH + 1) - 1
        B, S, D = x.shape
        flat_x = x.reshape(B * S, D)
        T = flat_x.shape[0]
        current = jnp.zeros((T,), dtype=jnp.int32)
        all_nodes = []
        all_logits = []
        for _ in range(DEPTH + 1):
            all_nodes.append(current)
            score = jnp.einsum('td,td->t', flat_x, w1s[current]) + b1s[current]
            all_logits.append(score)
            choice = ((jnp.sign(score) + 1.0) / 2.0).astype(jnp.int32)
            current = current * 2 + choice + 1
        logits = jnp.stack(all_logits, axis=1)
        path_weights = jax.nn.gelu(jnp.abs(logits), approximate=False)
        out = jnp.zeros((T, OUTPUT_WIDTH), dtype=x.dtype)
        for i in range(DEPTH + 1):
            nodes_i = all_nodes[i]
            t_i = jnp.einsum('td,tdo->to', flat_x, w2s[nodes_i]) + b2s[nodes_i]
            out = out + t_i * path_weights[:, i][:, None]
        return out.reshape(B, S, OUTPUT_WIDTH)
    x = x + _L0_gnn_ref(_layernorm(x, axis=-1), L0_gnn_h_neigh, adj, adj, L0_gnn_Wq, L0_gnn_bq, L0_gnn_Wk, L0_gnn_bk, L0_gnn_Wv, L0_gnn_bv, L0_gnn_Wo, L0_gnn_bo, L0_gnn_E)
    x = x + _L0_ffn_ref(_layernorm(x, axis=-1)[None], L0_ffn_w1s, L0_ffn_b1s, L0_ffn_w2s, L0_ffn_b2s)[0]
    return x

_drawn_inputs = setup_inputs


def setup_inputs(seed=0):
    import zlib

    import numpy as np

    out = dict(_drawn_inputs(seed))
    spreads = {'L0_gnn_bq': (0.0, 0.1),
     'L0_gnn_bk': (0.0, 0.1),
     'L0_gnn_bv': (0.0, 0.1),
     'L0_gnn_bo': (0.0, 0.1),
     'L0_ffn_b1s': (0.0, 0.1),
     'L0_ffn_b2s': (0.0, 0.1)}
    factors = {}
    for name, (base, spread) in spreads.items():
        noise = np.random.default_rng([zlib.crc32(name.encode()), seed]).standard_normal(out[name].shape)
        drawn = base * np.exp(spread * noise) if base else spread * noise
        out[name] = jnp.asarray(drawn.astype(out[name].dtype))
    for name, factor in factors.items():
        out[name] = (out[name] * factor).astype(out[name].dtype)
    return out
```

```python
from contextlib import ExitStack

import concourse.bass as bass
from concourse import mybir

F32 = mybir.dt.float32
I32 = mybir.dt.int32
ALU = mybir.AluOpType
ACT = mybir.ActivationFunctionType

P = 128
N_TOK = 512
N_NEIGH = 512
D = 128
HEADS = 8
DH = D // HEADS
TILES = N_TOK // P
NT = N_NEIGH // P
DEPTH = 7
LEVELS = DEPTH + 1
NODES = 2 ** LEVELS - 1
NODES_PAD = 2 ** LEVELS
QUAD = 32
GROUP = P // QUAD
GROUPS = HEADS // GROUP
EPS = 1e-5
MASKED = 1e9
SCALE = float(DH) ** -0.5
RING = 4
DVE_HEADS = (0, 2, 4, 6, 7)
ACT_HEADS = (1, 3, 5)
PAIR = 2
UNITS = PAIR * HEADS
W2_PARTS = 4
NPG = 4
NODE_GROUPS = NODES_PAD // NPG


def nth(t, unit):
    return UNITS * (t + 1) + unit + 1


def wait_moved(eng, moved_dve, moved_act, t, unit):
    turn, unit = (t, unit) if unit >= 0 else (t - 1, unit + UNITS)
    tile, h = divmod(unit, HEADS)
    sem, mine = (moved_dve, DVE_HEADS) if h in DVE_HEADS else (moved_act, ACT_HEADS)
    eng.wait_ge(sem, PAIR * len(mine) * (turn + 1) + len(mine) * tile + mine.index(h) + 1)


def gnn_ffn_kernel(nc, x, adj, neigh_t, w_t, bq, bk, bv, bo, edge, w1_t, b1, w2_t, b2, out):
    with ExitStack() as ctx:
        def sb(name, shape, dt=F32):
            return ctx.enter_context(nc.sbuf_tensor(name, shape, dt))

        def ps(name):
            return ctx.enter_context(nc.psum_tensor(name, [P, 512], F32))

        def sem(name):
            return ctx.enter_context(nc.semaphore(name))

        w2 = sb("w2", [P, NODES_PAD, D])
        x_sb = sb("x_sb", [P, TILES, D])
        adj_sb = sb("adj_sb", [P, TILES, N_NEIGH], I32)
        mask_all = adj_sb[:].bitcast(F32)
        mask = sb("mask", [P, PAIR, N_NEIGH])
        neigh = sb("neigh", [P, N_NEIGH])
        msg = sb("msg", [P, N_NEIGH])
        w_sb = sb("w_sb", [P, 4, D])
        w_pad = sb("w_pad", [P, 2, GROUPS * P])
        rows = sb("rows", [6, P])
        cols = sb("cols", [P, 6])
        vrow = sb("vrow", [1, 4 * 256])
        w1_sb = sb("w1_sb", [P, NODES_PAD])
        b2_sb = sb("b2_sb", [P, 2, D])
        ident = sb("ident", [P, P])
        ones = sb("ones", [1, P])
        mhalf = sb("mhalf", [P, TILES])
        stats = sb("stats", [P, TILES, 6])
        mv = sb("mv", [P, TILES, 2])
        veps = sb("veps", [P, TILES])
        rstd = sb("rstd", [P, TILES])
        h_sb = sb("h_sb", [P, TILES, D])
        h_t = sb("h_t", [P, N_TOK])
        q_t = sb("q_t", [P, GROUPS, N_TOK])
        k_t = sb("k_t", [P, GROUPS, N_NEIGH])
        q_cur = sb("q_cur", [P, PAIR, GROUPS, P])
        v_sb = sb("v_sb", [P, NT, D])
        prob = sb("prob", [P, RING, N_NEIGH])
        prob_t = sb("prob_t", [P, 2, NT, P])
        negmax_cur = sb("negmax_cur", [P, PAIR, HEADS])
        negmax = sb("negmax", [P, TILES, HEADS])
        psums = sb("psums", [P, TILES, HEADS])
        live = sb("live", [P, TILES, HEADS])
        o_sb = sb("o_sb", [P, TILES, D])
        o_t = sb("o_t", [P, N_TOK])
        x1 = sb("x1", [P, TILES, D])
        right = sb("right", [P, TILES, NODES_PAD])
        path = sb("path", [P, TILES, NODES_PAD])
        coef = sb("coef", [P, TILES, NODES_PAD])
        coef_t = prob[:, 0:2, :]

        s_ps = ctx.enter_context(nc.psum_tensor("s_ps", [P, GROUP, 512], F32))
        turn_ps = [ps(f"turn_ps{i}") for i in range(2)]
        o_ps = ps("o_ps")
        misc_ps = ps("misc_ps")

        x_in, adj_in, w_in, neigh_in = sem("x_in"), sem("adj_in"), sem("w_in"), sem("neigh_in")
        bias_in, w1_in = sem("bias_in"), sem("w1_in")
        w2_in = [sem(f"w2_in{i}") for i in range(W2_PARTS)]
        rows_zero, consts, mask_ready, vstep, wpad_ready = (
            sem("rows_zero"), sem("consts"), sem("mask_ready"), sem("vstep"), sem("wpad_ready"))
        veps_ready, rstd_ready, h_ready = sem("veps_ready"), sem("rstd_ready"), sem("h_ready")
        pe_setup, dve_setup = sem("pe_setup"), sem("dve_setup")
        q_copied, scored, masked, exped, turned, moved_dve, moved_act, summed = (
            sem("q_copied"), sem("scored"), sem("masked"), sem("exped"), sem("turned"),
            sem("moved_dve"), sem("moved_act"), sem("summed"))
        pe_tail, dve_tail, act_tail = sem("pe_tail"), sem("dve_tail"), sem("act_tail")
        right_ready = sem("right_ready")
        max_kept, mask_built = sem("max_kept"), sem("mask_built")
        noded, weighed = sem("noded"), sem("weighed")
        final, stored = sem("final"), sem("stored")

        block = ctx.enter_context(nc.Block())

        @block.sync
        def _(sp):
            sp.dma_start(x_sb[:], x.rearrange("(t p) d -> p t d", p=P)).then_inc(x_in, 16)
            sp.dma_start(neigh[:], neigh_t).then_inc(neigh_in, 16)
            sp.dma_start(adj_sb[:], adj.rearrange("(t p) n -> p t n", p=P)).then_inc(adj_in, 16)
            sp.dma_start(w1_sb[:, 0:NODES], w1_t).then_inc(w1_in, 16)
            per = NODES_PAD // W2_PARTS
            for i in range(W2_PARTS):
                n0, n1 = i * per, min((i + 1) * per, NODES)
                sp.dma_start(w2[:, n0:n1, :], w2_t[:, n0 * D:n1 * D].rearrange("p (n o) -> p n o", o=D)
                             ).then_inc(w2_in[i], 16)
            sp.wait_ge(final, 1)
            sp.dma_start(out.rearrange("(t p) d -> p t d", p=P), x1[:]).then_inc(stored, 16)
            sp.wait_ge(stored, 16)

        @block.gpsimd
        def _(pool):
            nc.gpsimd.memset(rows[:], 0.0).then_inc(rows_zero, 1)
            nc.gpsimd.memset(b2_sb[:], 0.0).then_inc(rows_zero, 1)
            nc.gpsimd.memset(ident[:], 0.0).then_inc(consts, 1)
            pool.wait_ge(consts, 1)
            nc.gpsimd.affine_select(out=ident[:], in_=ident[:], compare_op=ALU.not_equal, fill=1.0,
                                    base=0, pattern=[[-1, P]], channel_multiplier=1).then_inc(consts, 1)
            nc.gpsimd.memset(ones[:], 1.0).then_inc(consts, 1)
            nc.gpsimd.memset(mhalf[:], -0.5).then_inc(consts, 1)
            nc.gpsimd.memset(w_pad[:], 0.0).then_inc(wpad_ready, 1)
            pool.wait_ge(wpad_ready, 1)
            pool.wait_ge(w_in, 16)
            for i in range(2):
                nc.gpsimd.tensor_copy(w_pad[:, i, :].rearrange("p (h c) -> p h c", c=QUAD)[:, :, 0:DH],
                                      w_sb[:, i, :].rearrange("p (h c) -> p h c", c=DH)
                                      ).then_inc(wpad_ready, 1)
            pool.wait_ge(veps_ready, 1)
            nc.gpsimd.tensor_tensor(rstd[:], veps[:], mhalf[:], ALU.pow).then_inc(rstd_ready, 1)
            nc.gpsimd.memset(w2[:, NODES:NODES_PAD, :], 0.0).then_inc(consts, 1)
            nc.gpsimd.memset(coef[:, :, NODES:NODES_PAD], 0.0).then_inc(consts, 1)
            nc.gpsimd.memset(path[:, :, 0:1], 1.0).then_inc(consts, 1)
            pool.wait_ge(adj_in, 16)
            nc.gpsimd.tensor_scalar(mask_all[:], adj_sb[:], 0.0, MASKED, ALU.is_equal, ALU.mult
                                    ).then_inc(mask_built, 1)
            pool.wait_ge(mask_built, 1)
            pool.wait_ge(dve_setup, 6)
            with pool.Fori(0, TILES // PAIR) as t:
                for s in range(PAIR):
                    pool.wait_ge(scored, nth(t, HEADS * (s + 1) - 1 - UNITS))
                    nc.gpsimd.tensor_copy(q_cur[:, s], q_t[:, :, bass.ds(t * (PAIR * P) + s * P, P)]
                                          ).then_inc(q_copied, 1)
                    pool.wait_ge(masked, nth(t, HEADS * (s + 1) - 1 - UNITS))
                    nc.gpsimd.tensor_copy(mask[:, s], mask_all[:, bass.ds(t * PAIR + s, 1), :
                                          ].rearrange("p a n -> p (a n)")).then_inc(mask_ready, 1)
            pool.wait_ge(veps_ready, 2)
            nc.gpsimd.tensor_tensor(rstd[:], veps[:], mhalf[:], ALU.pow).then_inc(rstd_ready, 1)

        @block.scalar
        def _(act):
            act.dma_start(w_sb[:], w_t.rearrange("p (m o) -> p m o", m=4)).then_inc(w_in, 16)
            act.dma_start(vrow[:, 0:D], bv.rearrange("(a n) -> a n", a=1)).then_inc(bias_in, 16)
            act.dma_start(vrow[:, D:2 * D], bo.rearrange("(a n) -> a n", a=1)).then_inc(bias_in, 16)
            act.dma_start(vrow[:, 2 * D:2 * D + NODES], b1.rearrange("(a n) -> a n", a=1)).then_inc(bias_in, 16)
            act.wait_ge(rows_zero, 2)
            act.dma_start(b2_sb[:, 0, :], b2[0:P, :]).then_inc(bias_in, 16)
            act.dma_start(b2_sb[0:NODES - P, 1, :], b2[P:NODES, :]).then_inc(bias_in, 16)
            for i, b in enumerate((bq, bk)):
                act.dma_start(rows[2 * i:2 * i + 2, :].rearrange("g (j c) -> g j c", c=QUAD)[:, :, 0:DH],
                              b.rearrange("(g j c) -> g j c", g=GROUPS, c=DH)).then_inc(bias_in, 16)
            act.dma_start(rows[4:6, :], edge).then_inc(bias_in, 16)
            act.preload_act_table(ACT.Exp)
            with act.Fori(0, TILES // PAIR) as t:
                for u in range(UNITS):
                    s, h = divmod(u, HEADS)
                    act.wait_ge(masked, nth(t, u))
                    nc.scalar.activation(prob[:, u % RING, :], prob[:, u % RING, :], ACT.Exp,
                                         bias=negmax_cur[:, s, h:h + 1], scale=-1.0,
                                         accum_out=psums[:, bass.ds(t * PAIR + s, 1), h:h + 1
                                                         ].rearrange("p a b -> p (a b)")).then_inc(exped, 1)
                    if (u - 1) % HEADS in ACT_HEADS and u >= 1:
                        act.wait_ge(turned, nth(t, u - 1))
                        act.wait_ge(summed, nth(t, u - 3))
                        nc.scalar.activation(prob_t[:, (u - 1) % 2].rearrange("p m t -> p (m t)"),
                                             turn_ps[(u - 1) % 2][:], ACT.Copy).then_inc(moved_act, 1)
            act.wait_ge(right_ready, 1)
            nc.scalar.activation(coef[:, :, 0:NODES], s_ps[:, :, 0:NODES], ACT.Abs).then_inc(act_tail, 1)
            act.wait_ge(act_tail, 1)
            nc.scalar.activation(coef[:, :, 0:NODES], coef[:, :, 0:NODES], ACT.Gelu).then_inc(act_tail, 1)

        @block.tensor
        def _(pe):
            pe.wait_ge(consts, 4)
            pe.wait_ge(bias_in, 16 * 8)
            nc.tensor.transpose(misc_ps[:, 0:6], rows[:], ident[0:6, 0:6]).then_inc(pe_setup, 1)
            pe.wait_ge(h_ready, 1)
            for t in range(TILES):
                last = nc.tensor.transpose(turn_ps[0][:, t * P:(t + 1) * P], h_sb[:, t, :], ident[:])
            last.then_inc(pe_setup, 1)
            pe.wait_ge(wpad_ready, 3)
            pe.wait_ge(dve_setup, 2)
            for g in range(GROUPS):
                last = nc.tensor.matmul(s_ps[:, g, :], w_pad[:, 1, g * P:(g + 1) * P], msg[:],
                                        start=True, stop=True)
            last.then_inc(pe_setup, 1)
            for m in range(NT):
                nc.tensor.matmul(turn_ps[1][:, m * D:(m + 1) * D], msg[:, m * P:(m + 1) * P], w_sb[:, 2, :],
                                 start=True, stop=False)
                last = nc.tensor.matmul(turn_ps[1][:, m * D:(m + 1) * D], ones[:], vrow[:, 0:D],
                                        start=False, stop=True)
            last.then_inc(pe_setup, 1)
            pe.wait_ge(dve_setup, 3)
            for g in range(GROUPS):
                last = nc.tensor.matmul(s_ps[:, 2 + g, :], w_pad[:, 0, g * P:(g + 1) * P], h_t[:],
                                        start=True, stop=True)
            last.then_inc(pe_setup, 1)
            pe.wait_ge(dve_setup, 7)
            with pe.Fori(0, TILES // PAIR) as t:
                def scores(u):
                    s, h = divmod(u, HEADS)
                    g, j = divmod(h, GROUP)
                    lo = QUAD * j
                    if h == 0:
                        pe.wait_ge(q_copied, PAIR * t + s + 1)
                    pe.wait_ge(masked, nth(t, u - GROUP))
                    nc.tensor.matmul(s_ps[:, j, :], q_cur[lo:lo + DH, s, g, :], k_t[lo:lo + DH, g, :],
                                     start=True, stop=True).then_inc(scored, 1)

                def weighted_values(u):
                    s, h = divmod(u, HEADS)
                    wait_moved(pe, moved_dve, moved_act, t, u)
                    for m in range(NT):
                        last = nc.tensor.matmul(o_ps[:, bass.ds(t * (PAIR * D) + (s * D + h * DH), DH)],
                                                prob_t[:, u % 2, m, :],
                                                v_sb[:, m, h * DH:(h + 1) * DH],
                                                start=(m == 0), stop=(m == NT - 1))
                    last.then_inc(summed, 1)

                for u in range(GROUP):
                    scores(u)
                for u in range(UNITS):
                    pe.wait_ge(exped, nth(t, u))
                    wait_moved(pe, moved_dve, moved_act, t, u - 2)
                    for m in range(NT):
                        last = nc.tensor.transpose(turn_ps[u % 2][:, m * P:(m + 1) * P],
                                                   prob[:, u % RING, m * P:(m + 1) * P], ident[:])
                    last.then_inc(turned, 1)
                    if u + GROUP < UNITS:
                        scores(u + GROUP)
                    if u >= 1:
                        weighted_values(u - 1)
                weighted_values(UNITS - 1)

            pe.wait_ge(dve_tail, 3)
            for t in range(TILES):
                last = nc.tensor.transpose(turn_ps[0][:, t * P:(t + 1) * P], o_sb[:, t, :], ident[:])
            last.then_inc(pe_tail, 1)
            pe.wait_ge(dve_tail, 4)
            for t in range(TILES):
                nc.tensor.matmul(misc_ps[:, t * D:(t + 1) * D], o_t[:, t * P:(t + 1) * P], w_sb[:, 3, :],
                                 start=True, stop=False)
                last = nc.tensor.matmul(misc_ps[:, t * D:(t + 1) * D], ones[:], vrow[:, D:2 * D],
                                        start=False, stop=True)
            last.then_inc(pe_tail, 1)
            pe.wait_ge(h_ready, 2)
            for t in range(TILES):
                last = nc.tensor.transpose(turn_ps[1][:, t * P:(t + 1) * P], h_sb[:, t, :], ident[:])
            last.then_inc(pe_tail, 1)
            pe.wait_ge(dve_tail, 6)
            pe.wait_ge(w1_in, 16)
            for t in range(TILES):
                nc.tensor.matmul(s_ps[:, t, 0:NODES], h_t[:, t * P:(t + 1) * P], w1_sb[:, 0:NODES],
                                 start=True, stop=False)
                last = nc.tensor.matmul(s_ps[:, t, 0:NODES], ones[:], vrow[:, 2 * D:2 * D + NODES],
                                        start=False, stop=True)
                last.then_inc(pe_tail, 1) if t == 0 else None
            last.then_inc(pe_tail, 1)
            pe.wait_ge(dve_tail, 7)
            for c in range(2):
                for t in range(TILES):
                    last = nc.tensor.transpose(turn_ps[c][:, t * P:(t + 1) * P], coef[:, t, c * P:(c + 1) * P],
                                               ident[:])
            last.then_inc(pe_tail, 1)
            pe.wait_ge(dve_tail, 9)
            for t in range(TILES):
                for c in range(2):
                    last = nc.tensor.matmul(misc_ps[:, t * D:(t + 1) * D], coef_t[:, c, t * P:(t + 1) * P],
                                            b2_sb[:, c, :], start=(c == 0), stop=(c == 1))
            last.then_inc(pe_tail, 1)
            for i in range(W2_PARTS):
                pe.wait_ge(w2_in[i], 16)
            pe.wait_ge(consts, 7)
            with pe.Fori(0, NODE_GROUPS) as g:
                for t in range(TILES):
                    pe.wait_ge(weighed, NPG * TILES * g + t + 1)
                    nc.tensor.matmul(s_ps[:, t, :], h_t[:, t * P:(t + 1) * P],
                                     w2[:, bass.ds(g * NPG, NPG), :].rearrange("p n o -> p (n o)"),
                                     start=True, stop=True).then_inc(noded, 1)

        @block.vector
        def _(dve):
            steps = [0]

            def then(ins):
                steps[0] += 1
                ins.then_inc(vstep, 1)
                dve.wait_ge(vstep, steps[0])

            def normalise(src, nth):
                for t in range(TILES):
                    ins = nc.vector.bn_stats(stats[:, t, :], src[:, t, :])
                then(ins)
                for t in range(TILES):
                    ins = nc.vector.bn_aggr(mv[:, t, :], stats[:, t, :])
                then(ins)
                nc.vector.tensor_scalar(veps[:], mv[:, :, 1], EPS, None, ALU.add).then_inc(veps_ready, 1)
                dve.wait_ge(rstd_ready, nth)
                for t in range(TILES):
                    ins = nc.vector.tensor_scalar(h_sb[:, t, :], src[:, t, :], mv[:, t, 0:1],
                                                  rstd[:, t:t + 1], ALU.subtract, ALU.mult)
                ins.then_inc(h_ready, 1)

            for unit_sem in (scored, masked, exped, turned, summed):
                dve.sem_inc(unit_sem, UNITS)
            dve.sem_inc(moved_dve, PAIR * len(DVE_HEADS))
            dve.sem_inc(moved_act, PAIR * len(ACT_HEADS))
            dve.sem_inc(weighed, TILES)
            dve.wait_ge(x_in, 16)
            normalise(x_sb, 1)
            dve.wait_ge(pe_setup, 1)
            nc.vector.tensor_copy(cols[:], misc_ps[:, 0:6]).then_inc(dve_setup, 1)
            dve.wait_ge(dve_setup, 1)
            dve.wait_ge(neigh_in, 16)
            nc.vector.tensor_scalar(msg[:], neigh[:], cols[:, 5:6], None, ALU.add).then_inc(dve_setup, 1)
            dve.wait_ge(pe_setup, 2)
            nc.vector.tensor_copy(h_t[:], turn_ps[0][:]).then_inc(dve_setup, 1)
            dve.wait_ge(pe_setup, 3)
            for g in range(GROUPS):
                ins = nc.vector.tensor_scalar(k_t[:, g, :], s_ps[:, g, :], cols[:, 2 + g:3 + g], None, ALU.add)
            ins.then_inc(dve_setup, 1)
            dve.wait_ge(pe_setup, 4)
            nc.vector.tensor_copy(v_sb[:], turn_ps[1][:].rearrange("p (m d) -> p m d", d=D)).then_inc(dve_setup, 1)
            dve.wait_ge(pe_setup, 5)
            for g in range(GROUPS):
                ins = nc.vector.tensor_scalar(q_t[:, g, :], s_ps[:, 2 + g, :], cols[:, g:g + 1], -SCALE,
                                              ALU.add, ALU.mult)
            ins.then_inc(dve_setup, 2)
            with dve.Fori(0, TILES // PAIR) as t:
                for u in range(UNITS + 1):
                    s, h = divmod(u, HEADS)
                    if u < UNITS:
                        if h == 0:
                            dve.wait_ge(mask_ready, PAIR * t + s + 1)
                        dve.wait_ge(scored, nth(t, u))
                        dve.wait_ge(turned, nth(t, u - RING))
                        dve.nop(nofuse=True)
                        nc.vector.tensor_tensor_reduce(out=prob[:, u % RING, :], in0=s_ps[:, h % GROUP, :],
                                                       in1=mask[:, s, :], scale=1.0, scalar=3.0e38,
                                                       op0=ALU.add, op1=ALU.min,
                                                       accum_out=negmax_cur[:, s, h:h + 1]).then_inc(masked, 1)
                    if u >= 1 and (u - 1) % HEADS in DVE_HEADS:
                        dve.wait_ge(turned, nth(t, u - 1))
                        dve.wait_ge(summed, nth(t, u - 3))
                        nc.vector.tensor_copy(prob_t[:, (u - 1) % 2].rearrange("p m t -> p (m t)"),
                                              turn_ps[(u - 1) % 2][:]).then_inc(moved_dve, 1)
                dve.wait_ge(masked, nth(t, UNITS - 1))
                nc.vector.tensor_copy(negmax[:, bass.ds(t * PAIR, PAIR), :], negmax_cur[:]).then_inc(max_kept, 1)
                dve.wait_ge(max_kept, t + 1)

            dve.wait_ge(exped, UNITS + HEADS * TILES)
            dve.wait_ge(max_kept, TILES // PAIR)
            nc.vector.reciprocal(psums[:], psums[:]).then_inc(dve_tail, 1)
            nc.vector.tensor_scalar(live[:], negmax[:], 0.5 * MASKED, None, ALU.is_lt).then_inc(dve_tail, 1)
            dve.wait_ge(dve_tail, 2)
            then(nc.vector.tensor_tensor(live[:], live[:], psums[:], ALU.mult))
            dve.wait_ge(summed, UNITS + HEADS * TILES)
            nc.vector.tensor_tensor(o_sb[:].rearrange("p t (h c) -> p (t h) c", c=DH),
                                    o_ps[:].rearrange("p (h c) -> p h c", c=DH),
                                    live[:].rearrange("p t h -> p (t h)").unsqueeze(2).to_broadcast(
                                        [P, TILES * HEADS, DH]), ALU.mult).then_inc(dve_tail, 1)
            dve.wait_ge(pe_tail, 1)
            nc.vector.tensor_copy(o_t[:], turn_ps[0][:]).then_inc(dve_tail, 1)
            dve.wait_ge(pe_tail, 2)
            nc.vector.tensor_tensor(x1[:], x_sb[:], misc_ps[:].rearrange("p (t d) -> p t d", d=D), ALU.add
                                    ).then_inc(dve_tail, 1)
            dve.wait_ge(dve_tail, 5)
            normalise(x1, 2)
            dve.wait_ge(pe_tail, 3)
            nc.vector.tensor_copy(h_t[:], turn_ps[1][:]).then_inc(dve_tail, 1)
            dve.wait_ge(pe_tail, 5)
            dve.wait_ge(consts, 7)
            nc.vector.tensor_scalar(right[:, :, 0:NODES], s_ps[:, :, 0:NODES], 0.0, None, ALU.is_gt
                                    ).then_inc(right_ready, 1)
            dve.wait_ge(right_ready, 1)
            for l in range(DEPTH):
                n, at = 2 ** l, 2 ** l - 1
                child = path[:, :, 2 * at + 1:2 * at + 1 + 2 * n].rearrange("p t (n c) -> p t n c", c=2)
                then(nc.vector.tensor_tensor(child[:, :, :, 1], path[:, :, at:at + n],
                                             right[:, :, at:at + n], ALU.mult))
                then(nc.vector.tensor_tensor(child[:, :, :, 0], path[:, :, at:at + n],
                                             child[:, :, :, 1], ALU.subtract))
            dve.wait_ge(act_tail, 2)
            nc.vector.tensor_tensor(coef[:, :, 0:NODES], coef[:, :, 0:NODES], path[:, :, 0:NODES], ALU.mult
                                    ).then_inc(dve_tail, 1)
            dve.wait_ge(pe_tail, 6)
            for c in range(2):
                nc.vector.tensor_copy(coef_t[:, c, :], turn_ps[c][:]).then_inc(dve_tail, 1)
            dve.wait_ge(pe_tail, 7)
            then(nc.vector.tensor_tensor(x1[:], x1[:], misc_ps[:].rearrange("p (t d) -> p t d", d=D), ALU.add))
            with dve.Fori(0, NODE_GROUPS) as g:
                for i in range(NPG):
                    for t in range(TILES):
                        if i == 0:
                            dve.wait_ge(noded, TILES * g + t + 1)
                        dve.wait_ge(weighed, NPG * TILES * g + TILES * i + t + 1)
                        nc.vector.scalar_tensor_tensor(out=x1[:, t, :], in0=s_ps[:, t, i * D:(i + 1) * D],
                                                       scalar=coef[:, t, bass.ds(g * NPG + i, 1)],
                                                       in1=x1[:, t, :], op0=ALU.mult, op1=ALU.add
                                                       ).then_inc(weighed, 1)
            dve.wait_ge(weighed, TILES * (NODES_PAD + 1))
            dve.sem_inc(final, 1)


_INS = ("x", "adj", "neigh_t", "w_t", "bq", "bk", "bv", "bo", "edge", "w1_t", "b1", "w2_t", "b2")


def kernel(**inputs):
    import numpy as np
    import concourse.bacc as bacc
    from concourse.bass_utils import run_bass_kernel_spmd as run

    g = {k: np.asarray(v) for k, v in inputs.items()}
    laid = {
        "x": g["x"],
        "adj": g["adj"],
        "neigh_t": g["L0_gnn_h_neigh"].T,
        "w_t": np.concatenate([g[f"L0_gnn_W{m}"].T for m in "qkvo"], axis=1),
        "bq": g["L0_gnn_bq"], "bk": g["L0_gnn_bk"], "bv": g["L0_gnn_bv"], "bo": g["L0_gnn_bo"],
        "edge": g["L0_gnn_E"],
        "w1_t": g["L0_ffn_w1s"].T,
        "b1": g["L0_ffn_b1s"],
        "w2_t": g["L0_ffn_w2s"].transpose(1, 0, 2).reshape(D, NODES * D),
        "b2": g["L0_ffn_b2s"],
    }
    nc = bacc.Bacc("TRN2", target_bir_lowering=False, num_devices=1)
    arrays, args = {}, []
    for name in _INS:
        a = np.ascontiguousarray(laid[name])
        arrays[f"in_{name}"] = a
        args.append(nc.dram_tensor(f"in_{name}", a.shape, mybir.dt.from_np(a.dtype), kind="ExternalInput").ap())
    args.append(nc.dram_tensor("out_x", (N_TOK, D), F32, kind="ExternalOutput").ap())
    gnn_ffn_kernel(nc, *args)
    result = run(nc, [arrays], core_ids=[0])
    return result.results[0]["out_x"]
```

```python
from contextlib import ExitStack

import concourse.bass as bass
from concourse import mybir

F32 = mybir.dt.float32
I32 = mybir.dt.int32
F16 = mybir.dt.float16
BF16 = mybir.dt.bfloat16
AX_X = mybir.AxisListType.X
ALU = mybir.AluOpType
ACT = mybir.ActivationFunctionType

P = 128
N_TOK = 512
N_NEIGH = 512
D = 128
HEADS = 8
DH = D // HEADS
TILES = N_TOK // P
NT = N_NEIGH // P
UNITS = TILES * HEADS
DEPTH = 7
LEVELS = DEPTH + 1
NODES = 2 ** LEVELS - 1
NODES_PAD = 2 ** LEVELS
LEAVES = 2 ** DEPTH
LEAF0 = LEAVES - 1
EPS = 1e-5
MASKED = 1e9
SCALE = float(DH) ** -0.5
RING = 4
W2_PARTS = 4
HALF = 4
STEP = 2 * HALF
PARTS = 3
PAIRS = ((0, 0), (0, 1), (0, 2), (1, 0), (1, 1), (2, 0))
STACK = len(PAIRS) * DH
BIASES = 2 * D + NODES
BV, BO, B1 = 0, D, 2 * D


def list_entries(nc, engine, nodes, s, e):
    at = nc.s_assert_within(e + s * NODES_PAD, s * NODES_PAD, (s + 1) * NODES_PAD - STEP,
                            skip_runtime_bounds_check_because="e is a multiple of STEP below NODES_PAD")
    _, found = nc.values_load_multi_w_load_instructions(
        nodes[0:1, bass.ds(at, STEP)], engines=(engine,), min_val=0, max_val=NODES,
        skip_runtime_bounds_check_because="entries are node numbers, NODES past the list's end")
    return found


def gnn_ffn_kernel(nc, x, adj, neigh_t, w_t, cols, rows, w1_t, w2_t, b2, k_parts, q_parts, out):
    with ExitStack() as ctx:
        def sb(name, shape, dt=F32):
            return ctx.enter_context(nc.sbuf_tensor(name, shape, dt))

        def ps(name):
            return ctx.enter_context(nc.psum_tensor(name, [P, 512], F32))

        def sem(name):
            return ctx.enter_context(nc.semaphore(name))

        def view(tensor, lo, size, dt, pattern, **dims):
            return tensor.rearrange("p a n -> p (a n)").bitcast(dt)[:, lo:lo + size].rearrange(pattern, **dims)

        w2 = sb("w2", [P, NODES_PAD, D])
        x_sb = sb("x_sb", [P, TILES, D])
        mask = sb("mask", [P, TILES, N_NEIGH], BF16)
        msg = sb("msg", [P, N_NEIGH])
        w_sb = sb("w_sb", [P, 4, D])
        col_sb = sb("col_sb", [P, 4])
        row_sb = sb("row_sb", [1, BIASES])
        row_p = sb("row_p", [1, PARTS, BIASES], BF16)
        w1_sb = sb("w1_sb", [P, NODES])
        b2_sb = sb("b2_sb", [P, 2, D])
        ident = sb("ident", [P, P])
        ones = sb("ones", [1, P], BF16)
        ones_h = sb("ones_h", [P, P], F16)
        before = sb("before", [P, P], F16)
        upto = sb("upto", [P, P], F16)
        count_row = sb("count_row", [P, N_TOK], F16)
        node_col = sb("node_col", [P, 2], F16)
        token_col = sb("token_col", [P, TILES], F16)
        mhalf = sb("mhalf", [P, TILES])
        stats = sb("stats", [P, TILES, 6])
        mv = sb("mv", [P, TILES, 2])
        veps = sb("veps", [P, TILES])
        rstd = sb("rstd", [P, TILES])
        h_sb = sb("h_sb", [P, TILES, D])
        h_t = sb("h_t", [P, N_TOK])
        k_p = sb("k_p", [P, PARTS, N_NEIGH], BF16)
        q_p = sb("q_p", [P, PARTS, N_TOK], BF16)
        k_st = sb("k_st", [P, HEADS, N_NEIGH], BF16)
        q_st = sb("q_st", [P, HEADS, N_TOK], BF16)
        v_st = sb("v_st", [P, NT, HEADS, PARTS, DH], BF16)
        prob = sb("prob", [P, RING, N_NEIGH])
        prob_t = sb("prob_t", [P, 2, 2, N_NEIGH], F16)
        negmax = sb("negmax", [P, TILES, HEADS])
        psums = sb("psums", [P, TILES, HEADS])
        live = sb("live", [P, TILES, HEADS])
        o_sb = sb("o_sb", [P, TILES, D])
        o_t = sb("o_t", [P, N_TOK])
        x1 = sb("x1", [P, TILES, D])
        right = sb("right", [P, TILES, NODES_PAD], F16)
        path = sb("path", [P, TILES, NODES_PAD], F16)
        path_s = sb("path_s", [P, TILES, NODES_PAD], F16)
        picked = sb("picked", [P, TILES, LEVELS])
        picked_p = sb("picked_p", [P, TILES, PARTS, LEVELS], BF16)
        rest8 = sb("rest8", [P, 2, TILES, LEVELS])
        weight_s = sb("weight_s", [P, TILES, LEVELS])
        leaf_count = sb("leaf_count", [P, P], F16)
        pos = sb("pos", [P, TILES])
        active_h = sb("active_h", [P, 2, TILES], F16)
        active = sb("active", [P, 2 * TILES])
        rank = sb("rank", [P, 2 * TILES])
        entries = sb("entries", [1, TILES], I32)
        token_s = sb("token_s", [P, TILES], I32)

        adj_sb = prob[:].bitcast(I32)
        k_f, q_f, v_f = o_t[:], x1[:].rearrange("p t d -> p (t d)"), o_sb[:].rearrange("p t d -> p (t d)")
        perm = view(prob[:], 0, TILES * N_TOK, F16, "p (t s) -> p t s", s=N_TOK)
        chosen = view(prob[:], TILES * N_TOK, 2 * TILES * NODES_PAD, F16, "p (c k) -> p c k", c=2)
        prod = view(k_st[:], 0, TILES * NODES_PAD, F32, "p (t n) -> p t n", n=NODES_PAD)
        coef = view(k_st[:], TILES * NODES_PAD, TILES * NODES_PAD, F32, "p (t n) -> p t n", n=NODES_PAD)
        h_p = view(q_st[:], 0, TILES * 2 * D, F16, "p (t i d) -> p t i d", i=2, d=D)
        x1_p = view(q_st[:], TILES * 2 * D, TILES * PARTS * D, BF16, "p (t i d) -> p t i d", i=PARTS, d=D)
        place_l = view(q_st[:], TILES * 3 * D, TILES * LEAVES, F32, "p (t n) -> p t n", n=LEAVES)
        nodes = view(mask[0:1], 0, TILES * NODES_PAD, I32, "p (a n) -> p (a n)", a=1)
        coef_t = prob_t[:].rearrange("p a b n -> p (a b n)").bitcast(F32).rearrange("p (c n) -> p c n", c=2)
        hs_t = msg
        acc = [x_sb, o_sb, h_sb, view(k_p[:], 0, TILES * D, F32, "p (t d) -> p t d", d=D)]
        result = x1

        s_ps = ctx.enter_context(nc.psum_tensor("s_ps", [P, 4, 512], F32))
        score_ps = [s_ps[:, i, :] for i in range(2)]
        o_ps = [s_ps[:, 2 + i, 0:HEADS * PARTS * DH] for i in range(2)]
        turn_ps = [ps(f"turn_ps{i}") for i in range(2)]
        aux_ps = ps("aux_ps")
        misc_ps = ps("misc_ps")

        product_ps = [[s_ps[:, j, 0:D] for j in range(HALF)],
                      [b[:, 0:D] for b in (turn_ps[0], turn_ps[1], aux_ps, misc_ps)]]

        x_in, adj_in, w_in, neigh_in = sem("x_in"), sem("adj_in"), sem("w_in"), sem("neigh_in")
        col_in, row_in, b2_zero, b2_in, w1_in = (
            sem("col_in"), sem("row_in"), sem("b2_zero"), sem("b2_in"), sem("w1_in"))
        w2_in = [sem(f"w2_in{i}") for i in range(W2_PARTS)]
        consts, consts2, msg_ready, mask_ready = sem("consts"), sem("consts2"), sem("msg_ready"), sem("mask_ready")
        veps_ready, rstd_ready, h_ready, ht_ready = (
            sem("veps_ready"), sem("rstd_ready"), sem("h_ready"), sem("ht_ready"))
        row_split, k_split, q_split, v_split = sem("row_split"), sem("k_split"), sem("q_split"), sem("v_split")
        k_done, h_turned, v_done, q_done = sem("k_done"), sem("h_turned"), sem("v_done"), sem("q_done")
        k_out, q_out, k_stacked, q_stacked = sem("k_out"), sem("q_out"), sem("k_stacked"), sem("q_stacked")
        scored, masked, exped, turned, hi_moved, lo_moved, summed = (
            sem("scored"), sem("masked"), sem("exped"), sem("turned"), sem("hi_moved"), sem("lo_moved"),
            sem("summed"))
        o_moved = sem("o_moved")
        vstep = sem("vstep")
        live_ready, o_ready, o_turned, ot_ready, projected, x1_ready = (
            sem("live_ready"), sem("o_ready"), sem("o_turned"), sem("ot_ready"), sem("projected"), sem("x1_ready"))
        h_split, x1_split, node_scored, path_ready, leaves_counted, leaf_count_ready = (
            sem("h_split"), sem("x1_split"), sem("node_scored"), sem("path_ready"), sem("leaves_counted"),
            sem("leaf_count_ready"))
        placed, perm_ready, path_sorted, path_s_ready, h_sorted, hs_ready = (
            sem("placed"), sem("perm_ready"), sem("path_sorted"), sem("path_s_ready"), sem("h_sorted"),
            sem("hs_ready"))
        tokens_sorted, counted, active_ready, ranked, chosen_ready, listed, lists_ready = (
            sem("tokens_sorted"), sem("counted"), sem("active_ready"), sem("ranked"), sem("chosen_ready"),
            sem("listed"), sem("lists_ready"))
        picked_ready, weighted, picked_split, weight_sorted, coef_ready, coef_turned, coef_t_ready = (
            sem("picked_ready"), sem("weighted"), sem("picked_split"), sem("weight_sorted"), sem("coef_ready"),
            sem("coef_turned"), sem("coef_t_ready"))
        x1_sorted, biased, acc_ready, acc_zero = sem("x1_sorted"), sem("biased"), sem("acc_ready"), sem("acc_zero")
        multiplied = [sem(f"multiplied{t}") for t in range(TILES)]
        added = [sem(f"added{t}") for t in range(TILES)]
        tile_added, tile_done, stored = sem("tile_added"), sem("tile_done"), sem("stored")

        block = ctx.enter_context(nc.Block())

        def stack(eng, dst, src, which, stacked):
            for r, pair in enumerate(PAIRS):
                eng.dma_start(dst[r * DH:(r + 1) * DH], src[pair[which]].rearrange("(h c) n -> c h n", c=DH)
                              ).then_inc(stacked, 16)

        @block.sync
        def _(sp):
            sp.dma_start(msg[:], neigh_t).then_inc(neigh_in, 16)
            sp.dma_start(x_sb[:], x.rearrange("(t p) d -> p t d", p=P)).then_inc(x_in, 16)
            sp.dma_start(adj_sb, adj.rearrange("(t p) n -> p t n", p=P)).then_inc(adj_in, 16)
            sp.wait_ge(k_split, 2 * PARTS)
            sp.dma_start(k_parts.rearrange("i p n -> p i n"), k_p[:]).then_inc(k_out, 16)
            sp.wait_ge(k_out, 16)
            stack(sp, k_st, k_parts, 1, k_stacked)
            sp.wait_ge(q_split, 2 * PARTS)
            sp.dma_start(q_parts.rearrange("i p n -> p i n"), q_p[:]).then_inc(q_out, 16)
            sp.wait_ge(q_out, 16)
            stack(sp, q_st, q_parts, 0, q_stacked)
            per = NODES_PAD // W2_PARTS
            for i in range(W2_PARTS):
                n0, n1 = i * per, min((i + 1) * per, NODES)
                sp.dma_start(w2[:, n0:n1, :], w2_t[:, n0 * D:n1 * D].rearrange("p (n o) -> p n o", o=D)
                             ).then_inc(w2_in[i], 16)

        @block.gpsimd
        def _(pool):
            nc.gpsimd.memset(ident[:], 0.0).then_inc(consts, 1)
            nc.gpsimd.memset(mhalf[:], -0.5).then_inc(consts, 1)
            nc.gpsimd.memset(ones[:], 1.0).then_inc(consts, 1)
            pool.wait_ge(consts, 1)
            nc.gpsimd.affine_select(out=ident[:], in_=ident[:], compare_op=ALU.not_equal, fill=1.0,
                                    base=0, pattern=[[-1, P]], channel_multiplier=1).then_inc(consts, 1)
            nc.gpsimd.memset(b2_sb[:], 0.0).then_inc(b2_zero, 1)
            pool.wait_ge(consts, 4)
            pool.wait_ge(veps_ready, 1)
            nc.gpsimd.tensor_tensor(rstd[:], veps[:], mhalf[:], ALU.pow).then_inc(rstd_ready, 1)
            pool.wait_ge(row_in, 16)
            for i in range(PARTS):
                nc.gpsimd.tensor_copy(row_p[:, i], row_sb[:]).then_inc(row_split, 1)
                pool.wait_ge(row_split, 2 * i + 1)
                nc.gpsimd.tensor_tensor(row_sb[:], row_sb[:], row_p[:, i], ALU.subtract).then_inc(row_split, 1)
                pool.wait_ge(row_split, 2 * i + 2)
            nc.gpsimd.memset(ones_h[:], 1.0).then_inc(consts2, 1)
            nc.gpsimd.memset(w2[:, NODES:NODES_PAD, :], 0.0).then_inc(consts2, 1)
            nc.gpsimd.memset(path[:], 0.0).then_inc(consts2, 1)
            nc.gpsimd.memset(upto[:], 1.0).then_inc(consts2, 1)
            nc.gpsimd.memset(before[:], 1.0).then_inc(consts2, 1)
            pool.wait_ge(consts2, 5)
            nc.gpsimd.memset(path[:, :, 0:1], 1.0).then_inc(consts2, 1)
            nc.gpsimd.affine_select(out=upto[:], in_=upto[:], compare_op=ALU.is_ge, fill=0.0,
                                    base=0, pattern=[[1, P]], channel_multiplier=-1).then_inc(consts2, 1)
            nc.gpsimd.affine_select(out=before[:], in_=before[:], compare_op=ALU.is_gt, fill=0.0,
                                    base=0, pattern=[[1, P]], channel_multiplier=-1).then_inc(consts2, 1)
            nc.gpsimd.iota(count_row[:], [[1, N_TOK]], base=0, channel_multiplier=0,
                           allow_small_or_imprecise_dtypes=True).then_inc(consts2, 1)
            nc.gpsimd.iota(node_col[:], [[P, 2]], base=-NODES, channel_multiplier=1,
                           allow_small_or_imprecise_dtypes=True).then_inc(consts2, 1)
            nc.gpsimd.iota(token_col[:], [[P, TILES]], base=0, channel_multiplier=1,
                           allow_small_or_imprecise_dtypes=True).then_inc(consts2, 1)
            pool.wait_ge(veps_ready, 2)
            nc.gpsimd.tensor_tensor(rstd[:], veps[:], mhalf[:], ALU.pow).then_inc(rstd_ready, 1)
            pool.wait_ge(h_split, 2)
            pool.wait_ge(h_turned, 2)
            nc.gpsimd.memset(acc[2][:], 0.0).then_inc(acc_zero, 1)
            nc.gpsimd.memset(acc[3][:], 0.0).then_inc(acc_zero, 1)
            for t in range(TILES):
                pool.wait_ge(tile_done, t + 1)
                nc.gpsimd.indirect_dma_start(out=out, out_offset=bass.IndirectOffsetOnAxis(
                    ap=token_s[:, t:t + 1], axis=0), in_=result[:, t, :], in_offset=None).then_inc(stored, 16)
            pool.wait_ge(stored, 16 * TILES)

        @block.scalar
        def _(act):
            act.dma_start(w_sb[:], w_t.rearrange("p (m o) -> p m o", m=4)).then_inc(w_in, 16)
            act.dma_start(col_sb[:], cols).then_inc(col_in, 16)
            act.dma_start(row_sb[:], rows).then_inc(row_in, 16)
            act.dma_start(w1_sb[:], w1_t).then_inc(w1_in, 16)
            act.wait_ge(b2_zero, 1)
            act.dma_start(b2_sb[:, 0, :], b2[0:P, :]).then_inc(b2_in, 16)
            act.dma_start(b2_sb[0:NODES - P, 1, :], b2[P:NODES, :]).then_inc(b2_in, 16)
            act.preload_act_table(ACT.Exp)
            act.wait_ge(v_done, 1)
            nc.scalar.activation(v_f, turn_ps[1][:], ACT.Copy).then_inc(v_split, 1)
            for i in range(PARTS):
                act.wait_ge(v_split, 2 * i + 1)
                nc.scalar.activation(v_st[:, :, :, i, :].rearrange("p m h c -> p (m h) c"),
                                     v_f.rearrange("p (a c) -> p a c", c=DH), ACT.Copy).then_inc(v_split, 1)
            for u in range(UNITS + 1):
                if u < UNITS:
                    t, h = divmod(u, HEADS)
                    act.wait_ge(masked, u + 1)
                    nc.scalar.activation(prob[:, u % RING, :], prob[:, u % RING, :], ACT.Exp,
                                         bias=negmax[:, t, h:h + 1], scale=-1.0,
                                         accum_out=psums[:, t, h:h + 1]).then_inc(exped, 1)
                if u >= 1:
                    v = u - 1
                    act.wait_ge(turned, v + 1)
                    if v >= 2:
                        act.wait_ge(summed, v - 1)
                    nc.scalar.activation(prob_t[:, v % 2, 0, :], turn_ps[v % 2][:], ACT.Copy).then_inc(hi_moved, 1)
            act.preload_act_table(ACT.Gelu)
            act.wait_ge(o_turned, 1)
            nc.scalar.activation(o_t[:], turn_ps[0][:], ACT.Copy).then_inc(ot_ready, 1)
            act.wait_ge(h_turned, 2)
            nc.scalar.activation(h_t[:], turn_ps[1][:], ACT.Copy).then_inc(ht_ready, 1)
            act.wait_ge(picked_ready, 1)
            nc.scalar.activation(picked[:], picked[:], ACT.Abs).then_inc(weighted, 1)
            act.wait_ge(weighted, 1)
            nc.scalar.activation(picked[:], picked[:], ACT.Gelu).then_inc(weighted, 1)
            act.wait_ge(path_sorted, 1)
            nc.scalar.activation(path_s[:], s_ps[:, 2:4, :].rearrange("p b (s n) -> p (b s) n", n=NODES_PAD),
                                 ACT.Copy).then_inc(path_s_ready, 1)
            act.wait_ge(h_sorted, 1)
            nc.scalar.activation(hs_t[:], turn_ps[1][:], ACT.Copy).then_inc(hs_ready, 1)
            act.wait_ge(x1_sorted, 1)
            nc.scalar.activation(acc[0][:].rearrange("p t d -> p (t d)"), turn_ps[0][:], ACT.Copy
                                 ).then_inc(acc_ready, 1)
            for c in range(2):
                act.wait_ge(coef_turned, c + 1)
                nc.scalar.activation(coef_t[:, c, :], (turn_ps[1], misc_ps)[c][:], ACT.Copy
                                     ).then_inc(coef_t_ready, 1)

        @block.tensor
        def _(pe):
            def transposes(bank, src, done):
                for t in range(TILES):
                    last = nc.tensor.transpose(bank[:, t * P:(t + 1) * P], src[:, t, :], ident[:])
                last.then_inc(done, 1)

            def add_bias(dst, at, n):
                for i in range(PARTS):
                    last = nc.tensor.matmul(dst, ones[:], row_p[:, i, at:at + n], start=False, stop=(i == PARTS - 1))
                return last

            pe.wait_ge(consts, 4)
            pe.wait_ge(w_in, 16)
            pe.wait_ge(msg_ready, 1)
            nc.tensor.matmul(aux_ps[:], w_sb[:, 1, :], msg[:], start=True, stop=True).then_inc(k_done, 1)
            pe.wait_ge(h_ready, 1)
            transposes(turn_ps[0], h_sb, h_turned)
            pe.wait_ge(ht_ready, 1)
            nc.tensor.matmul(misc_ps[:], w_sb[:, 0, :], h_t[:], start=True, stop=True).then_inc(q_done, 1)
            pe.wait_ge(row_split, 2 * PARTS - 1)
            for m in range(NT):
                dst = turn_ps[1][:, m * D:(m + 1) * D]
                nc.tensor.matmul(dst, msg[:, m * P:(m + 1) * P], w_sb[:, 2, :], start=True, stop=False)
                last = add_bias(dst, BV, D)
            last.then_inc(v_done, 1)

            def scores(u):
                t, h = divmod(u, HEADS)
                if u >= 2:
                    pe.wait_ge(masked, u - 1)
                nc.tensor.matmul(score_ps[u % 2], q_st[0:STACK, h, t * P:(t + 1) * P], k_st[0:STACK, h, :],
                                 start=True, stop=True).then_inc(scored, 1)

            def weighted_values(u):
                t, h = divmod(u, HEADS)
                pe.wait_ge(lo_moved, u + 1)
                if h == 0 and t >= 2:
                    pe.wait_ge(o_moved, t - 1)
                for i in range(2):
                    for m in range(NT):
                        last = nc.tensor.matmul(o_ps[t % 2][:, h * PARTS * DH:(h + 1) * PARTS * DH],
                                                prob_t[:, u % 2, i, m * P:(m + 1) * P],
                                                v_st[:, m, h].rearrange("p i c -> p (i c)"),
                                                start=(i == 0 and m == 0), stop=(i == 1 and m == NT - 1))
                last.then_inc(summed, 1)

            pe.wait_ge(k_stacked, 16 * len(PAIRS))
            pe.wait_ge(q_stacked, 16 * len(PAIRS))
            scores(0)
            scores(1)
            for u in range(UNITS):
                pe.wait_ge(exped, u + 1)
                if u >= 2:
                    pe.wait_ge(lo_moved, u - 1)
                if u < 2:
                    pe.wait_ge((ht_ready, v_split)[u], 1)
                for m in range(NT):
                    last = nc.tensor.transpose(turn_ps[u % 2][:, m * P:(m + 1) * P],
                                               prob[:, u % RING, m * P:(m + 1) * P], ident[:])
                last.then_inc(turned, 1)
                if u + 2 < UNITS:
                    scores(u + 2)
                if u == 1:
                    pe.wait_ge(v_split, 2 * PARTS)
                if u >= 1:
                    weighted_values(u - 1)
            weighted_values(UNITS - 1)

            pe.wait_ge(o_ready, 1)
            transposes(turn_ps[0], o_sb, o_turned)
            pe.wait_ge(ot_ready, 1)
            for t in range(TILES):
                dst = misc_ps[:, t * D:(t + 1) * D]
                nc.tensor.matmul(dst, o_t[:, t * P:(t + 1) * P], w_sb[:, 3, :], start=True, stop=False)
                last = add_bias(dst, BO, D)
            last.then_inc(projected, 1)
            pe.wait_ge(h_ready, 2)
            transposes(turn_ps[1], h_sb, h_turned)
            pe.wait_ge(ht_ready, 2)
            pe.wait_ge(w1_in, 16)
            for t in range(TILES):
                dst = s_ps[:, t // 2, (t % 2) * NODES_PAD:(t % 2) * NODES_PAD + NODES]
                nc.tensor.matmul(dst, h_t[:, t * P:(t + 1) * P], w1_sb[:], start=True, stop=False)
                last = add_bias(dst, B1, NODES)
            last.then_inc(node_scored, 1)

            pe.wait_ge(consts2, 11)
            pe.wait_ge(path_ready, 1)
            for t in range(TILES):
                last = nc.tensor.matmul(aux_ps[:, 0:1], path[:, t, LEAF0:NODES], ones_h[:, 0:1],
                                        start=(t == 0), stop=(t == TILES - 1))
            last.then_inc(leaves_counted, 1)
            pe.wait_ge(leaf_count_ready, 1)
            for t in range(TILES):
                dst = turn_ps[0][:, t * LEAVES:(t + 1) * LEAVES]
                nc.tensor.matmul(dst, leaf_count[:], before[:], start=True, stop=False)
                for other in range(t):
                    nc.tensor.matmul(dst, ones_h[:], path[:, other, LEAF0:NODES], start=False, stop=False)
                last = nc.tensor.matmul(dst, before[:], path[:, t, LEAF0:NODES], start=False, stop=True)
            last.then_inc(placed, 1)

            def by_order(dst, s, values, stop=True):
                n = len(values(0))
                for t in range(TILES):
                    for i, value in enumerate(values(t)):
                        last = nc.tensor.matmul(dst, perm[:, t, s * P:(s + 1) * P], value,
                                                start=(t == 0 and i == 0), stop=(t == TILES - 1 and i == n - 1))
                return last

            pe.wait_ge(perm_ready, 1)
            for s in range(TILES):
                last = by_order(s_ps[:, 2 + s // 2, (s % 2) * NODES_PAD:(s % 2 + 1) * NODES_PAD], s,
                                lambda t: [path[:, t, :]])
            last.then_inc(path_sorted, 1)
            pe.wait_ge(h_split, 2)
            for t in range(TILES):
                for i in range(2):
                    last = nc.tensor.matmul(turn_ps[1][:], h_p[:, t, i, :], perm[:, t, :],
                                            start=(t == 0 and i == 0), stop=(t == TILES - 1 and i == 1))
            last.then_inc(h_sorted, 1)
            for s in range(TILES):
                last = by_order(misc_ps[:, s:s + 1], s, lambda t: [token_col[:, t:t + 1]])
            last.then_inc(tokens_sorted, 1)
            pe.wait_ge(path_s_ready, 1)
            for c in range(2):
                for s in range(TILES):
                    last = nc.tensor.matmul(aux_ps[:, c * TILES + s:c * TILES + s + 1],
                                            path_s[:, s, c * P:(c + 1) * P], ones_h[:, 0:1],
                                            start=True, stop=True)
            last.then_inc(counted, 1)
            pe.wait_ge(active_ready, 1)
            nc.tensor.matmul(misc_ps[:, 0:TILES], upto[:], active_h[:, 0, :], start=True, stop=True)
            nc.tensor.matmul(misc_ps[:, TILES:2 * TILES], ones_h[:], active_h[:, 0, :], start=True, stop=False)
            nc.tensor.matmul(misc_ps[:, TILES:2 * TILES], upto[:], active_h[:, 1, :], start=False, stop=True)
            for c in range(2):
                last = nc.tensor.matmul(misc_ps[0:1, 2 * TILES:3 * TILES], ones_h[:, 0:1], active_h[:, c, :],
                                        start=(c == 0), stop=(c == 1))
            last.then_inc(ranked, 1)
            pe.wait_ge(x1_split, 2 * PARTS - 1)
            for s in range(TILES):
                last = by_order(turn_ps[0][:, s * D:(s + 1) * D], s,
                                lambda t: [x1_p[:, t, i, :] for i in range(PARTS)])
            last.then_inc(x1_sorted, 1)
            pe.wait_ge(chosen_ready, 1)
            for half in range(2):
                for c in range(2):
                    last = nc.tensor.matmul(s_ps[0:1, half, :], node_col[:, c:c + 1],
                                            chosen[:, c, half * 512:(half + 1) * 512],
                                            start=(c == 0), stop=(c == 1))
            last.then_inc(listed, 1)
            pe.wait_ge(picked_split, 2 * PARTS - 1)
            for s in range(TILES):
                last = by_order(aux_ps[:, s * PARTS * LEVELS:(s + 1) * PARTS * LEVELS], s,
                                lambda t: [picked_p[:, t].rearrange("p i l -> p (i l)")])
            last.then_inc(weight_sorted, 1)
            pe.wait_ge(coef_ready, 1)
            pe.wait_ge(hs_ready, 1)
            for c in range(2):
                transposes((turn_ps[1], misc_ps)[c], coef[:, :, c * P:(c + 1) * P], coef_turned)
            pe.wait_ge(coef_t_ready, 2)
            pe.wait_ge(b2_in, 32)
            for s in range(TILES):
                for c in range(2):
                    last = nc.tensor.matmul(aux_ps[:, s * D:(s + 1) * D], coef_t[:, c, s * P:(s + 1) * P],
                                            b2_sb[:, c, :], start=(c == 0), stop=(c == 1))
            last.then_inc(biased, 1)

            for i in range(W2_PARTS):
                pe.wait_ge(w2_in[i], 16)
            pe.wait_ge(lists_ready, 2)
            pe.wait_ge(acc_ready, 2)
            for s in range(TILES):
                n_entries = pe.value_load(entries[0:1, s:s + 1], min_val=LEVELS, max_val=NODES)
                if s >= 1:
                    pe.wait_ge(tile_added, s)
                with pe.Fori(0, n_entries, STEP) as e:
                    found = list_entries(nc, pe.engine, nodes, s, e)
                    for half in range(2):
                        pe.wait_ge(added[s], e + HALF * (half + 1))
                        for j in range(HALF):
                            last = nc.tensor.matmul(product_ps[half][j], hs_t[:, s * P:(s + 1) * P],
                                                    w2[:, bass.ds(found[HALF * half + j], 1), :
                                                       ].rearrange("p n o -> p (n o)"), start=True, stop=True)
                        last.then_inc(multiplied[s], HALF)

        @block.vector
        def _(dve):
            steps = [0]

            def then(ins):
                steps[0] += 1
                ins.then_inc(vstep, 1)
                dve.wait_ge(vstep, steps[0])

            def statistics(src):
                for t in range(TILES):
                    ins = nc.vector.bn_stats(stats[:, t, :], src[:, t, :])
                then(ins)
                for t in range(TILES):
                    ins = nc.vector.bn_aggr(mv[:, t, :], stats[:, t, :])
                then(ins)
                nc.vector.tensor_scalar(veps[:], mv[:, :, 1], EPS, None, ALU.add).then_inc(veps_ready, 1)

            def normalise(src, nth):
                dve.wait_ge(rstd_ready, nth)
                for t in range(TILES):
                    ins = nc.vector.tensor_scalar(h_sb[:, t, :], src[:, t, :], mv[:, t, 0:1],
                                                  rstd[:, t:t + 1], ALU.subtract, ALU.mult)
                ins.then_inc(h_ready, 1)

            def split(src, parts, done, at=0):
                for i in range(len(parts)):
                    nc.vector.tensor_copy(parts[i], src).then_inc(done, 1)
                    at += 1
                    if i < len(parts) - 1:
                        dve.wait_ge(done, at)
                        nc.vector.tensor_tensor(src, src, parts[i], ALU.subtract).then_inc(done, 1)
                        at += 1
                        dve.wait_ge(done, at)

            for s in range(TILES):
                dve.sem_inc(added[s], STEP)
            dve.wait_ge(neigh_in, 16)
            dve.wait_ge(col_in, 16)
            nc.vector.tensor_scalar(msg[:], msg[:], col_sb[:, 3:4], None, ALU.add).then_inc(msg_ready, 1)
            dve.wait_ge(x_in, 16)
            statistics(x_sb)
            dve.wait_ge(k_done, 1)
            nc.vector.tensor_scalar(k_f, aux_ps[:], col_sb[:, 1:2], None, ALU.add).then_inc(k_split, 1)
            dve.wait_ge(k_split, 1)
            normalise(x_sb, 1)
            split(k_f, [k_p[:, i, :] for i in range(PARTS)], k_split, 1)
            dve.wait_ge(h_turned, 1)
            nc.vector.tensor_copy(h_t[:], turn_ps[0][:]).then_inc(ht_ready, 1)
            dve.wait_ge(adj_in, 16)
            nc.vector.tensor_scalar(mask[:], adj_sb, 0.0, MASKED, ALU.is_equal, ALU.mult).then_inc(mask_ready, 1)
            dve.wait_ge(q_done, 1)
            nc.vector.tensor_scalar(q_f, misc_ps[:], col_sb[:, 0:1], -SCALE, ALU.add, ALU.mult).then_inc(q_split, 1)
            dve.wait_ge(q_split, 1)
            split(q_f, [q_p[:, i, :] for i in range(PARTS)], q_split, 1)
            for i in range(PARTS - 1):
                dve.wait_ge(v_split, 2 * i + 2)
                nc.vector.tensor_tensor(v_f.rearrange("p (a c) -> p a c", c=DH),
                                        v_f.rearrange("p (a c) -> p a c", c=DH),
                                        v_st[:, :, :, i, :].rearrange("p m h c -> p (m h) c"),
                                        ALU.subtract).then_inc(v_split, 1)
            dve.wait_ge(mask_ready, 1)
            for u in range(UNITS + 1):
                if u < UNITS:
                    t, h = divmod(u, HEADS)
                    dve.wait_ge(scored, u + 1)
                    if u >= RING:
                        dve.wait_ge(turned, u - RING + 1)
                    nc.vector.tensor_tensor_reduce(out=prob[:, u % RING, :], in0=score_ps[u % 2],
                                                   in1=mask[:, t, :], scale=1.0, scalar=3.0e38,
                                                   op0=ALU.add, op1=ALU.min,
                                                   accum_out=negmax[:, t, h:h + 1]).then_inc(masked, 1)
                if u >= 1:
                    v = u - 1
                    dve.wait_ge(hi_moved, v + 1)
                    nc.vector.tensor_tensor(prob_t[:, v % 2, 1, :], turn_ps[v % 2][:], prob_t[:, v % 2, 0, :],
                                            ALU.subtract).then_inc(lo_moved, 1)
                if u >= HEADS + 1 and u % HEADS == 1 or u == UNITS:
                    t = u // HEADS - 1
                    dve.wait_ge(summed, HEADS * (t + 1))
                    nc.vector.tensor_reduce(o_sb[:, t, :].rearrange("p (h c) -> p h c", c=DH),
                                            o_ps[t % 2].rearrange("p (h i c) -> p h c i", i=PARTS, c=DH),
                                            AX_X, ALU.add).then_inc(o_moved, 1)

            dve.wait_ge(exped, UNITS)
            dve.wait_ge(masked, UNITS)
            nc.vector.reciprocal(psums[:], psums[:]).then_inc(live_ready, 1)
            nc.vector.tensor_scalar(live[:], negmax[:], 0.5 * MASKED, None, ALU.is_lt).then_inc(live_ready, 1)
            dve.wait_ge(live_ready, 2)
            then(nc.vector.tensor_tensor(live[:], live[:], psums[:], ALU.mult))
            dve.wait_ge(o_moved, TILES)
            by_head = o_sb[:].rearrange("p t (h c) -> p (t h) c", c=DH)
            nc.vector.tensor_tensor(by_head, by_head, live[:].rearrange("p t h -> p (t h)").unsqueeze(2
                                    ).to_broadcast([P, TILES * HEADS, DH]), ALU.mult).then_inc(o_ready, 1)
            dve.wait_ge(projected, 1)
            nc.vector.tensor_tensor(x1[:], x_sb[:], misc_ps[:].rearrange("p (t d) -> p t d", d=D), ALU.add
                                    ).then_inc(x1_ready, 1)
            dve.wait_ge(x1_ready, 1)
            statistics(x1)
            normalise(x1, 2)
            dve.wait_ge(h_ready, 2)
            nc.vector.tensor_copy(h_p[:, :, 0, :], h_sb[:]).then_inc(h_split, 1)
            dve.wait_ge(h_split, 1)
            nc.vector.tensor_tensor(h_p[:, :, 1, :], h_sb[:], h_p[:, :, 0, :], ALU.subtract).then_inc(h_split, 1)
            split(x1[:], [x1_p[:, :, i, :] for i in range(PARTS)], x1_split)
            node_scores = s_ps[:, 0:2, :].rearrange("p b (t n) -> p (b t) n", n=NODES_PAD)[:, :, 0:NODES]
            dve.wait_ge(node_scored, 1)
            dve.wait_ge(consts2, 11)
            then(nc.vector.tensor_scalar(right[:, :, 0:NODES], node_scores, 0.0, None, ALU.is_gt))
            for l in range(DEPTH):
                n, at = 2 ** l, 2 ** l - 1
                child = path[:, :, 2 * at + 1:2 * at + 1 + 2 * n].rearrange("p t (n c) -> p t n c", c=2)
                then(nc.vector.tensor_tensor(child[:, :, :, 1], path[:, :, at:at + n],
                                             right[:, :, at:at + n], ALU.mult))
                ins = nc.vector.tensor_tensor(child[:, :, :, 0], path[:, :, at:at + n],
                                              child[:, :, :, 1], ALU.subtract)
                if l < DEPTH - 1:
                    then(ins)
            ins.then_inc(path_ready, 1)
            dve.wait_ge(leaves_counted, 1)
            nc.vector.tensor_copy(leaf_count[:], aux_ps[:, 0:1].to_broadcast([P, P])).then_inc(leaf_count_ready, 1)
            dve.wait_ge(placed, 1)
            then(nc.vector.tensor_tensor(place_l[:], turn_ps[0][:].rearrange("p (t n) -> p t n", n=LEAVES),
                                         path[:, :, LEAF0:NODES], ALU.mult))
            then(nc.vector.tensor_reduce(pos[:], place_l[:], AX_X, ALU.add))
            for t in range(TILES):
                ins = nc.vector.tensor_scalar(perm[:, t, :], count_row[:], pos[:, t:t + 1], None, ALU.is_equal)
            ins.then_inc(perm_ready, 1)
            then(nc.vector.tensor_tensor(prod[:, :, 0:NODES], node_scores, path[:, :, 0:NODES], ALU.mult))
            for l in range(LEVELS):
                ins = nc.vector.tensor_reduce(picked[:, :, l], prod[:, :, 2 ** l - 1:2 ** (l + 1) - 1], AX_X, ALU.add)
            ins.then_inc(picked_ready, 1)
            dve.wait_ge(tokens_sorted, 1)
            nc.vector.tensor_copy(token_s[:], misc_ps[:, 0:TILES])
            dve.wait_ge(counted, 1)
            nc.vector.tensor_scalar(active_h[:].rearrange("p c t -> p (c t)"), aux_ps[:, 0:2 * TILES], 0.5, None,
                                    ALU.is_gt).then_inc(active_ready, 1)
            then(nc.vector.tensor_scalar(active[:], aux_ps[:, 0:2 * TILES], 0.5, None, ALU.is_gt))
            dve.wait_ge(ranked, 1)
            then(nc.vector.tensor_scalar(rank[:], misc_ps[:, 0:2 * TILES], -1.0, None, ALU.add))
            nc.vector.tensor_copy(entries[:], misc_ps[0:1, 2 * TILES:3 * TILES]).then_inc(lists_ready, 1)
            for c in range(2):
                for s in range(TILES):
                    i = c * TILES + s
                    ins = nc.vector.tensor_scalar(chosen[:, c, s * NODES_PAD:(s + 1) * NODES_PAD],
                                                  count_row[:, 0:NODES_PAD], rank[:, i:i + 1],
                                                  active[:, i:i + 1], ALU.is_equal, ALU.mult)
            ins.then_inc(chosen_ready, 1)
            dve.wait_ge(weighted, 2)
            split(picked[:], [picked_p[:, :, i, :] for i in range(PARTS)], picked_split)
            dve.wait_ge(listed, 1)
            nc.vector.tensor_scalar(nodes[:], s_ps[0:1, 0:2, :].rearrange("p a n -> p (a n)"), float(NODES), None,
                                    ALU.add).then_inc(lists_ready, 1)
            dve.wait_ge(weight_sorted, 1)
            parts = aux_ps[:, 0:TILES * PARTS * LEVELS].rearrange("p (s i l) -> p s l i", i=PARTS, l=LEVELS)
            then(nc.vector.tensor_reduce(weight_s[:], parts, AX_X, ALU.add))
            dve.wait_ge(path_s_ready, 1)
            for l in range(LEVELS):
                n = 2 ** l
                nc.vector.tensor_tensor(coef[:, :, n - 1:2 * n - 1], path_s[:, :, n - 1:2 * n - 1],
                                        weight_s[:, :, l:l + 1].to_broadcast([P, TILES, n]), ALU.mult)
            nc.vector.memset(coef[:, :, NODES:NODES_PAD], 0.0).then_inc(coef_ready, 1)
            dve.wait_ge(biased, 1)
            nc.vector.tensor_copy(acc[1][:].rearrange("p t d -> p (t d)"), aux_ps[:]).then_inc(acc_ready, 1)
            dve.wait_ge(acc_ready, 2)
            dve.wait_ge(acc_zero, 2)
            for s in range(TILES):
                n_entries = dve.value_load(entries[0:1, s:s + 1], min_val=LEVELS, max_val=NODES)
                with dve.Fori(0, n_entries, STEP) as e:
                    found = list_entries(nc, dve.engine, nodes, s, e)
                    for half in range(2):
                        dve.wait_ge(multiplied[s], e + HALF * (half + 1))
                        dve.wait_ge(added[s], e + (STEP + HALF * half))
                        for j in range(HALF):
                            ins = nc.vector.scalar_tensor_tensor(
                                out=acc[j][:, s, :], in0=product_ps[half][j],
                                scalar=coef[:, s, bass.ds(found[HALF * half + j], 1)],
                                in1=acc[j][:, s, :], op0=ALU.mult, op1=ALU.add)
                        ins.then_inc(added[s], HALF)
                dve.drain().then_inc(tile_added, 1)
                dve.wait_ge(tile_added, s + 1)
                then(nc.vector.tensor_tensor(acc[0][:, s, :], acc[0][:, s, :], acc[1][:, s, :], ALU.add))
                then(nc.vector.tensor_tensor(acc[2][:, s, :], acc[2][:, s, :], acc[3][:, s, :], ALU.add))
                nc.vector.tensor_tensor(result[:, s, :], acc[0][:, s, :], acc[2][:, s, :], ALU.add
                                        ).then_inc(tile_done, 1)


_INS = ("x", "adj", "neigh_t", "w_t", "cols", "rows", "w1_t", "w2_t", "b2")


def kernel(**inputs):
    import numpy as np
    import concourse.bacc as bacc
    from concourse.bass_utils import run_bass_kernel_spmd as run

    g = {k: np.asarray(v) for k, v in inputs.items()}
    laid = {
        "x": g["x"],
        "adj": g["adj"],
        "neigh_t": g["L0_gnn_h_neigh"].T,
        "w_t": np.concatenate([g[f"L0_gnn_W{m}"].T for m in "qkvo"], axis=1),
        "cols": np.stack([g["L0_gnn_bq"], g["L0_gnn_bk"], g["L0_gnn_E"][0], g["L0_gnn_E"][1]], axis=1),
        "rows": np.concatenate([g["L0_gnn_bv"], g["L0_gnn_bo"], g["L0_ffn_b1s"]])[None],
        "w1_t": g["L0_ffn_w1s"].T,
        "w2_t": g["L0_ffn_w2s"].transpose(1, 0, 2).reshape(D, NODES * D),
        "b2": g["L0_ffn_b2s"],
    }
    nc = bacc.Bacc("TRN2", target_bir_lowering=False, num_devices=1)
    arrays, args = {}, []
    for name in _INS:
        a = np.ascontiguousarray(laid[name])
        arrays[f"in_{name}"] = a
        args.append(nc.dram_tensor(f"in_{name}", a.shape, mybir.dt.from_np(a.dtype), kind="ExternalInput").ap())
    for name in ("k_parts", "q_parts"):
        args.append(nc.dram_tensor(name, (PARTS, D, 512), BF16, kind="Internal").ap())
    args.append(nc.dram_tensor("out_x", (N_TOK, D), F32, kind="ExternalOutput").ap())
    gnn_ffn_kernel(nc, *args)
    result = run(nc, [arrays], core_ids=[0])
    return result.results[0]["out_x"]
```

```python
from contextlib import ExitStack

import concourse.bass as bass
from concourse import mybir

F32 = mybir.dt.float32
I32 = mybir.dt.int32
F16 = mybir.dt.float16
BF16 = mybir.dt.bfloat16
AX_X = mybir.AxisListType.X
ALU = mybir.AluOpType
ACT = mybir.ActivationFunctionType

P = 128
N_TOK = 512
N_NEIGH = 512
D = 128
HEADS = 8
DH = D // HEADS
TILES = N_TOK // P
NT = N_NEIGH // P
UNITS = TILES * HEADS
DEPTH = 7
LEVELS = DEPTH + 1
NODES = 2 ** LEVELS - 1
NODES_PAD = 2 ** LEVELS
LEAVES = 2 ** DEPTH
LEAF0 = LEAVES - 1
EPS = 1e-5
MASKED = 1e9
SCALE = float(DH) ** -0.5
RING = 4
W2_PARTS = 4
HALF = 4
STEP = 2 * HALF
BY_DVE = (2, 3)
BY_ACT = STEP - sum(BY_DVE)
SUMS = STEP
SUMMED_AFTER = ((), (0, 1), (2,), (3,))
STORED_AFTER = ((), (), (0, 1), (2, 3))
LAG = 2
PARTS = 3
PAIRS = ((0, 0), (0, 1), (0, 2), (1, 0), (1, 1), (2, 0))
STACK = len(PAIRS) * DH
K_RUNS = ((0, 3, 0, 1), (3, 2, 0, 1), (5, 1, 0, 1))
Q_RUNS = ((0, 1, 0, 3), (3, 1, 1, 2), (5, 1, 2, 1))
Q_SLICES = ((0, P), (P, N_TOK))
TILE_SLICES = tuple((lo // P, hi // P) for lo, hi in Q_SLICES)
GROUPS = ((0, 2), (2, 4))
BIASES = 2 * D + NODES
BV, BO, B1 = 0, D, 2 * D


def list_entries(nc, engine, nodes, at):
    at = nc.s_assert_within(at, 0, TILES * NODES_PAD - STEP,
                            skip_runtime_bounds_check_because="at is a multiple of STEP inside the lists")
    _, found = nc.values_load_multi_w_load_instructions(
        nodes[0:1, bass.ds(at, STEP)], engines=(engine,), min_val=0, max_val=NODES,
        skip_runtime_bounds_check_because="entries are node numbers, NODES past the list's end")
    return found


def list_lengths(nc, engine, entries):
    _, lengths = nc.values_load_multi_w_load_instructions(
        entries[0:1, 0:TILES], engines=(engine,), min_val=STEP, max_val=NODES_PAD)
    return lengths


def tile_turns(nc, eng, lengths, nodes, turn, after):
    start = STEP
    for s in range(TILES):
        end = eng.snap(lengths[s] + start)
        with eng.Fori(start, end, STEP) as e:
            turn(s, list_entries(nc, eng.engine, nodes, e - start + s * NODES_PAD), e)
        after(s, end)
        start = end


def gnn_ffn_kernel(nc, x, adj, neigh_t, w_t, cols, rows, w1_t, w2_t, b2, k_parts, q_parts, x1_rows, out):
    with ExitStack() as ctx:
        def sb(name, shape, dt=F32):
            return ctx.enter_context(nc.sbuf_tensor(name, shape, dt))

        def ps(name):
            return ctx.enter_context(nc.psum_tensor(name, [P, 512], F32))

        def sem(name):
            return ctx.enter_context(nc.semaphore(name))

        def view(tensor, lo, size, dt, pattern, **dims):
            return tensor.rearrange("p a n -> p (a n)").bitcast(dt)[:, lo:lo + size].rearrange(pattern, **dims)

        w2 = sb("w2", [P, NODES_PAD, D])
        x_sb = sb("x_sb", [P, TILES, D])
        mask = sb("mask", [P, TILES, N_NEIGH], BF16)
        msg = sb("msg", [P, N_NEIGH])
        w_sb = sb("w_sb", [P, 4, D])
        col_sb = sb("col_sb", [P, 4])
        row_sb = sb("row_sb", [P, BIASES])
        w1_sb = sb("w1_sb", [P, NODES])
        b2_sb = sb("b2_sb", [P, 2, D])
        ident = sb("ident", [P, P])
        ones_h = sb("ones_h", [P, P], F16)
        before = sb("before", [P, P], F16)
        count_row = sb("count_row", [P, N_TOK], F16)
        tile_row = sb("tile_row", [P, TILES + 1])
        node_col = sb("node_col", [P, 2], F16)
        token_col = sb("token_col", [P, TILES], F16)
        mhalf = sb("mhalf", [P, TILES])
        stats = sb("stats", [P, TILES, 6])
        mv = sb("mv", [P, TILES, 2])
        veps = sb("veps", [P, TILES])
        rstd = sb("rstd", [P, TILES])
        row_pair = sb("row_pair", [P, 2, TILES * D])
        h_sb, o_sb = (row_pair[:, i, :].rearrange("p (t d) -> p t d", d=D) for i in range(2))
        h_t = sb("h_t", [P, N_TOK])
        early = sb("early", [P, 2 * HEADS + PARTS, N_NEIGH], BF16)
        k_st = early[:, 0:HEADS, :]
        q_st = early[:, HEADS:2 * HEADS, :]
        k_p = early[:, 2 * HEADS:, :]
        q_p = sb("q_p", [P, PARTS, N_TOK], BF16)
        v_st = sb("v_st", [P, NT, HEADS, PARTS, DH], BF16)
        prob = sb("prob", [P, RING, N_NEIGH])
        prob_t = sb("prob_t", [P, 2, 2, N_NEIGH], F16)
        negmax = sb("negmax", [P, TILES, HEADS])
        psums = sb("psums", [P, TILES, HEADS])
        live = sb("live", [P, TILES, HEADS])
        o_t = sb("o_t", [P, N_TOK])
        x1 = sb("x1", [P, TILES, D])
        sides = sb("sides", [P, TILES, LEAVES, 2], F16)
        path = sb("path", [P, TILES, NODES_PAD], F16)
        path_s = sb("path_s", [P, TILES, NODES_PAD], F16)
        picked = sb("picked", [P, TILES, LEVELS])
        picked_p = sb("picked_p", [P, TILES, PARTS, LEVELS], BF16)
        weight_s = sb("weight_s", [P, TILES, LEVELS])
        leaf_count = sb("leaf_count", [P, P], F16)
        pos = sb("pos", [P, TILES])
        from_tile = sb("from_tile", [P, TILES, TILES + 1], F16)
        coef = sb("coef", [P, TILES, NODES_PAD])
        turned_up = sb("turned_up", [1, TILES], I32)
        scaled_sb = sb("scaled_sb", [P, BY_ACT, D])
        active_h = sb("active_h", [P, 2, TILES], F16)
        active = sb("active", [P, 2 * TILES])
        rank = sb("rank", [P, 2 * TILES])
        counts_sb = sb("counts_sb", [P, 2, TILES + 1])
        entries = sb("entries", [1, TILES], I32)
        token_s = sb("token_s", [P, TILES], I32)

        adj_sb = prob[:].bitcast(I32)
        k_f, q_f, v_f = o_t[:], x1[:].rearrange("p t d -> p (t d)"), o_sb[:].rearrange("p t d -> p (t d)")
        perm = view(prob[:], 0, TILES * N_TOK, F16, "p (t s) -> p t s", s=N_TOK)
        chosen = view(prob[:], TILES * N_TOK, 2 * TILES * NODES_PAD, F16, "p (c k) -> p c k", c=2)
        nodes = view(row_pair[0:1], 0, TILES * NODES_PAD, I32, "p (a n) -> p (a n)", a=1)
        scores_b = view(mask[:], 0, TILES * NODES_PAD, F32, "p (t n) -> p t n", n=NODES_PAD)
        prod = prob_t[:].rearrange("p a b n -> p (a b n)").bitcast(F32).rearrange("p (t n) -> p t n", n=NODES_PAD)
        coef_t = prod.rearrange("p t n -> p (t n)").rearrange("p (c n) -> p c n", c=2)
        h_p = view(q_p[:], 0, TILES * 2 * D, F16, "p (t i d) -> p t i d", i=2, d=D)
        place_l = o_t[:].rearrange("p (t n) -> p t n", n=LEAVES)
        hs_t = msg
        acc = view(early[:], 0, (SUMS + 1) * TILES * D, F32, "p (j t d) -> p j t d", t=TILES, d=D)
        result = x1

        s_ps = ctx.enter_context(nc.psum_tensor("s_ps", [P, 4, 512], F32))
        score_ps = [s_ps[:, i, :] for i in range(2)]
        o_ps = [s_ps[:, 2 + i, 0:HEADS * PARTS * DH] for i in range(2)]
        turn_ps = [ps(f"turn_ps{i}") for i in range(2)]
        aux_ps = ps("aux_ps")
        misc_ps = ps("misc_ps")

        product_ps = [[s_ps[:, j, 0:D] for j in range(HALF)],
                      [b[:, 0:D] for b in (turn_ps[0], turn_ps[1], aux_ps, misc_ps)]]

        x_in, adj_in, w_in, neigh_in = sem("x_in"), sem("adj_in"), sem("w_in"), sem("neigh_in")
        col_in, row_in, b2_zero, b2_in, w1_in = (
            sem("col_in"), sem("row_in"), sem("b2_zero"), sem("b2_in"), sem("w1_in"))
        w2_in = [sem(f"w2_in{i}") for i in range(W2_PARTS)]
        consts, consts2, msg_ready, mask_ready = sem("consts"), sem("consts2"), sem("msg_ready"), sem("mask_ready")
        veps_ready, rstd_ready, h_ready, ht_ready = (
            sem("veps_ready"), sem("rstd_ready"), sem("h_ready"), sem("ht_ready"))
        x_biased, k_split, v_split = sem("x_biased"), sem("k_split"), sem("v_split")
        q_split, q_done, q_out, q_stacked = (
            [sem(f"{what}{i}") for i in range(len(Q_SLICES))] for what in ("q_split", "q_done", "q_out", "q_stacked"))
        k_done, h_turned, v_done = sem("k_done"), sem("h_turned"), sem("v_done")
        k_out, k_stacked = sem("k_out"), sem("k_stacked")
        scored, masked, exped, turned, hi_moved, lo_moved, summed = (
            sem("scored"), sem("masked"), sem("exped"), sem("turned"), sem("hi_moved"), sem("lo_moved"),
            sem("summed"))
        o_moved = sem("o_moved")
        vstep = sem("vstep")
        live_ready, o_ready, o_turned, ot_ready, projected, x1_ready = (
            sem("live_ready"), sem("o_ready"), sem("o_turned"), sem("ot_ready"), sem("projected"), sem("x1_ready"))
        h_split, x1_out, node_scored, path_ready, leaves_counted, leaf_count_ready = (
            sem("h_split"), sem("x1_out"), sem("node_scored"), sem("path_ready"), sem("leaves_counted"),
            sem("leaf_count_ready"))
        placed, perm_ready, path_sorted, path_s_ready, h_sorted, hs_ready = (
            sem("placed"), sem("perm_ready"), sem("path_sorted"), sem("path_s_ready"), sem("h_sorted"),
            sem("hs_ready"))
        pos_ready, counts_moved, tokens_moved = sem("pos_ready"), sem("counts_moved"), sem("tokens_moved")
        tokens_sorted, counted, active_ready, ranked, chosen_ready, listed, lists_ready = (
            sem("tokens_sorted"), sem("counted"), sem("active_ready"), sem("ranked"), sem("chosen_ready"),
            sem("listed"), sem("lists_ready"))
        picked_ready, weighted, picked_split, weight_sorted, coef_ready, coef_turned, coef_t_ready = (
            sem("picked_ready"), sem("weighted"), sem("picked_split"), sem("weight_sorted"), sem("coef_ready"),
            sem("coef_turned"), sem("coef_t_ready"))
        x1_sorted, biased, bias_moved, acc_zero = (
            sem("x1_sorted"), sem("biased"), sem("bias_moved"), sem("acc_zero"))
        multiplied, multiplied_last, added, scaled, pooled = (
            [sem(f"{what}{half}") for half in range(2)]
            for what in ("multiplied", "multiplied_last", "added", "scaled", "pooled"))
        tile_done, stored = sem("tile_done"), sem("stored")

        block = ctx.enter_context(nc.Block())

        def stack(eng, dst, src, runs, stacked, lo=0, hi=512):
            parts = src.rearrange("i (c h) n -> (i c) h n", h=HEADS)
            for r, n, i, times in runs:
                rows = parts[i * DH:(i + n) * DH, :, lo:hi]
                if times > 1:
                    rows = rows.unsqueeze(0).to_broadcast([times, n * DH, HEADS, hi - lo])
                eng.dma_start(dst[r * DH:(r + n * times) * DH, :, lo:hi], rows).then_inc(stacked, 16)

        def by_act(half):
            first = (HALF - BY_DVE[0]) * half
            return [(first + j - BY_DVE[half], j) for j in range(BY_DVE[half], HALF)]

        @block.sync
        def _(sp):
            sp.dma_start(msg[:], neigh_t).then_inc(neigh_in, 16)
            sp.dma_start(x_sb[:], x.rearrange("(t p) d -> p t d", p=P)).then_inc(x_in, 16)
            sp.dma_start(adj_sb, adj.rearrange("(t p) n -> p t n", p=P)).then_inc(adj_in, 16)
            sp.wait_ge(k_split, 2 * PARTS)
            sp.dma_start(k_parts.rearrange("i p n -> p i n"), k_p[:]).then_inc(k_out, 16)
            for i, (lo, hi) in enumerate(Q_SLICES):
                sp.wait_ge(q_split[i], 2 * PARTS)
                sp.dma_start(q_parts.rearrange("i p n -> p i n")[:, :, lo:hi], q_p[:, :, lo:hi]).then_inc(q_out[i], 16)
                if i == 0:
                    sp.wait_ge(k_out, 16)
                    stack(sp, k_st, k_parts, K_RUNS, k_stacked)
                sp.wait_ge(q_out[i], 16)
                stack(sp, q_st, q_parts, Q_RUNS, q_stacked[i], lo, hi)
            sp.wait_ge(k_stacked, 16 * len(K_RUNS))
            sp.wait_ge(b2_zero, 1)
            sp.dma_start(b2_sb[:, 0, :], b2[0:P, :]).then_inc(b2_in, 16)
            sp.dma_start(b2_sb[0:NODES - P, 1, :], b2[P:NODES, :]).then_inc(b2_in, 16)
            per = NODES_PAD // W2_PARTS
            for i in range(W2_PARTS):
                n0, n1 = i * per, min((i + 1) * per, NODES)
                sp.dma_start(w2[:, n0:n1, :], w2_t[:, n0 * D:n1 * D].rearrange("p (n o) -> p n o", o=D)
                             ).then_inc(w2_in[i], 16)

        @block.gpsimd
        def _(pool):
            nc.gpsimd.memset(ident[:], 0.0).then_inc(consts, 1)
            nc.gpsimd.memset(mhalf[:], -0.5).then_inc(consts, 1)
            pool.wait_ge(consts, 1)
            nc.gpsimd.affine_select(out=ident[:], in_=ident[:], compare_op=ALU.not_equal, fill=1.0,
                                    base=0, pattern=[[-1, P]], channel_multiplier=1).then_inc(consts, 1)
            nc.gpsimd.memset(b2_sb[:], 0.0).then_inc(b2_zero, 1)
            pool.wait_ge(consts, 3)
            for i, (t0, t1) in enumerate(TILE_SLICES):
                pool.wait_ge(veps_ready, i + 1)
                nc.gpsimd.tensor_tensor(rstd[:, t0:t1], veps[:, t0:t1], mhalf[:, t0:t1], ALU.pow
                                        ).then_inc(rstd_ready, 1)
            pool.wait_ge(row_in, 16)
            pool.wait_ge(h_ready, 2)
            nc.gpsimd.tensor_tensor(x_sb[:], x_sb[:], row_sb[:, BO:BO + D].unsqueeze(1).to_broadcast([P, TILES, D]),
                                    ALU.add).then_inc(x_biased, 1)
            for i in range(PARTS - 1):
                pool.wait_ge(v_split, 2 * i + 2)
                nc.gpsimd.tensor_tensor(v_f.rearrange("p (a c) -> p a c", c=DH),
                                        v_f.rearrange("p (a c) -> p a c", c=DH),
                                        v_st[:, :, :, i, :].rearrange("p m h c -> p (m h) c"),
                                        ALU.subtract).then_inc(v_split, 1)
            nc.gpsimd.memset(ones_h[:], 1.0).then_inc(consts2, 1)
            nc.gpsimd.memset(w2[:, NODES:NODES_PAD, :], 0.0).then_inc(consts2, 1)
            nc.gpsimd.memset(path[:], 0.0).then_inc(consts2, 1)
            nc.gpsimd.memset(before[:], 1.0).then_inc(consts2, 1)
            pool.wait_ge(consts2, 4)
            nc.gpsimd.memset(path[:, :, 0:1], 1.0).then_inc(consts2, 1)
            nc.gpsimd.affine_select(out=before[:], in_=before[:], compare_op=ALU.is_gt, fill=0.0,
                                    base=0, pattern=[[1, P]], channel_multiplier=-1).then_inc(consts2, 1)
            nc.gpsimd.iota(count_row[:], [[1, N_TOK]], base=0, channel_multiplier=0,
                           allow_small_or_imprecise_dtypes=True).then_inc(consts2, 1)
            nc.gpsimd.iota(tile_row[:], [[P, TILES + 1]], base=0, channel_multiplier=0,
                           allow_small_or_imprecise_dtypes=True).then_inc(consts2, 1)
            nc.gpsimd.iota(node_col[:], [[P, 2]], base=-NODES, channel_multiplier=1,
                           allow_small_or_imprecise_dtypes=True).then_inc(consts2, 1)
            nc.gpsimd.iota(token_col[:], [[P, TILES]], base=0, channel_multiplier=1,
                           allow_small_or_imprecise_dtypes=True).then_inc(consts2, 1)
            for i, (t0, t1) in enumerate(GROUPS):
                pool.wait_ge(veps_ready, 3 + i)
                nc.gpsimd.tensor_tensor(rstd[:, t0:t1], veps[:, t0:t1], mhalf[:, t0:t1], ALU.pow
                                        ).then_inc(rstd_ready, 1)
            pool.wait_ge(summed, UNITS)
            pool.wait_ge(lo_moved, UNITS)
            for i in range(len(Q_SLICES)):
                pool.wait_ge(q_stacked[i], 16 * len(Q_RUNS))
            pool.wait_ge(k_out, 16)
            nc.gpsimd.memset(acc[:, 1:SUMS], 0.0).then_inc(acc_zero, 1)
            for half in range(2):
                pool.sem_inc(pooled[half], STEP)
            pool.wait_ge(x1_out, 16)
            pool.wait_ge(tokens_moved, 1)
            for t in range(TILES):
                nc.gpsimd.indirect_dma_start(out=acc[:, 0, t, :], out_offset=None, in_=x1_rows,
                                             in_offset=bass.IndirectOffsetOnAxis(ap=token_s[:, t:t + 1], axis=0)
                                             ).then_inc(x1_sorted, 16)
            pool.wait_ge(lists_ready, 2)
            pool.wait_ge(acc_zero, 1)

            def add_scaled(s, found, e):
                for half in range(2):
                    pool.wait_ge(scaled[half], e + STEP)
                    pool.wait_ge(pooled[half], e)
                    for i, j in by_act(half):
                        mine = acc[:, half * HALF + j, s, :]
                        ins = nc.gpsimd.tensor_tensor(mine, mine, scaled_sb[:, i, :], ALU.add)
                    ins.then_inc(pooled[half], STEP)

            def store(s, end):
                for tile in STORED_AFTER[s]:
                    pool.wait_ge(tile_done, tile + 1)
                    nc.gpsimd.indirect_dma_start(out=out, out_offset=bass.IndirectOffsetOnAxis(
                        ap=token_s[:, tile:tile + 1], axis=0), in_=result[:, tile, :], in_offset=None
                                                 ).then_inc(stored, 16)

            tile_turns(nc, pool, list_lengths(nc, pool.engine, entries), nodes, add_scaled, store)
            pool.wait_ge(stored, 16 * TILES)

        @block.scalar
        def _(act):
            act.dma_start(col_sb[:], cols).then_inc(col_in, 16)
            act.dma_start(w_sb[:], w_t.rearrange("p (m o) -> p m o", m=4)).then_inc(w_in, 16)
            act.preload_act_table(ACT.Exp)
            act.dma_start(row_sb[:], rows.to_broadcast([P, BIASES])).then_inc(row_in, 16)
            act.dma_start(w1_sb[:], w1_t).then_inc(w1_in, 16)
            act.wait_ge(k_done, 1)
            nc.scalar.activation(k_f, aux_ps[:], ACT.Identity, bias=col_sb[:, 1:2]).then_inc(k_split, 1)
            for i in range(PARTS):
                act.wait_ge(k_split, 2 * i + 1)
                nc.scalar.activation(k_p[:, i, :], k_f, ACT.Copy).then_inc(k_split, 1)
            for i in range(PARTS):
                act.wait_ge(v_split, 2 * i + 1)
                nc.scalar.activation(v_st[:, :, :, i, :].rearrange("p m h c -> p (m h) c"),
                                     v_f.rearrange("p (a c) -> p a c", c=DH), ACT.Copy).then_inc(v_split, 1)
            for u in range(UNITS + LAG):
                if u >= LAG:
                    v = u - LAG
                    act.wait_ge(turned, v + 1)
                    if v >= 2:
                        act.wait_ge(summed, v - 1)
                    nc.scalar.activation(prob_t[:, v % 2, 0, :], turn_ps[v % 2][:], ACT.Copy).then_inc(hi_moved, 1)
                if u < UNITS:
                    t, h = divmod(u, HEADS)
                    act.wait_ge(masked, u + 1)
                    nc.scalar.activation(prob[:, u % RING, :], prob[:, u % RING, :], ACT.Exp,
                                         bias=negmax[:, t, h:h + 1], scale=-1.0,
                                         accum_out=psums[:, t, h:h + 1]).then_inc(exped, 1)
            act.preload_act_table(ACT.Gelu)
            for i, (t0, t1) in enumerate(GROUPS):
                act.wait_ge(o_turned, i + 1)
                nc.scalar.activation(o_t[:, t0 * P:t1 * P], turn_ps[i][:, t0 * P:t1 * P], ACT.Copy
                                     ).then_inc(ot_ready, 1)
            act.wait_ge(x1_ready, len(GROUPS))
            act.dma_start(x1_rows.rearrange("(t p) d -> p t d", p=P), x1[:]).then_inc(x1_out, 16)
            for i, (t0, t1) in enumerate(GROUPS):
                act.wait_ge(h_turned, 3 + i)
                nc.scalar.activation(h_t[:, t0 * P:t1 * P], turn_ps[i][:, t0 * P:t1 * P], ACT.Copy
                                     ).then_inc(ht_ready, 1)
            act.wait_ge(picked_ready, 1)
            nc.scalar.activation(picked[:], picked[:], ACT.Abs).then_inc(weighted, 1)
            act.wait_ge(weighted, 1)
            nc.scalar.activation(picked[:], picked[:], ACT.Gelu).then_inc(weighted, 1)
            act.wait_ge(path_sorted, 1)
            nc.scalar.activation(path_s[:], s_ps[:, 2:4, :].rearrange("p b (s n) -> p (b s) n", n=NODES_PAD),
                                 ACT.Copy).then_inc(path_s_ready, 1)
            act.wait_ge(listed, 1)
            nc.scalar.activation(nodes[:], s_ps[0:1, 0:2, :].rearrange("p a n -> p (a n)"), ACT.Copy,
                                 bias=float(NODES)).then_inc(lists_ready, 1)
            act.wait_ge(h_sorted, 1)
            nc.scalar.activation(hs_t[:], turn_ps[1][:], ACT.Copy).then_inc(hs_ready, 1)
            act.wait_ge(lists_ready, 2)
            lengths = list_lengths(nc, act.engine, entries)
            for c in range(2):
                act.wait_ge(coef_turned, c + 1)
                nc.scalar.activation(coef_t[:, c, :], (turn_ps[1], misc_ps)[c][:], ACT.Copy
                                     ).then_inc(coef_t_ready, 1)
            for half in range(2):
                act.sem_inc(scaled[half], STEP)

            def scale(s, found, e):
                for half in range(2):
                    act.wait_ge(multiplied_last[half], e)
                    act.wait_ge(pooled[half], e)
                    for i, j in by_act(half):
                        ins = nc.scalar.activation(scaled_sb[:, i, :], product_ps[half][j], ACT.Copy,
                                                   scale=coef[:, s, bass.ds(found[HALF * half + j], 1)])
                    ins.then_inc(scaled[half], STEP)

            def move_biases(s, end):
                if s < len(GROUPS):
                    t0, t1 = GROUPS[s]
                    act.wait_ge(biased, s + 1)
                    nc.scalar.activation(acc[:, SUMS, t0:t1], misc_ps[:, t0 * D:t1 * D].rearrange(
                        "p (t d) -> p t d", d=D), ACT.Copy).then_inc(bias_moved, 1)

            tile_turns(nc, act, lengths, nodes, scale, move_biases)

        @block.tensor
        def _(pe):
            def transposes(bank, src, done, t0=0, t1=TILES):
                for t in range(t0, t1):
                    last = nc.tensor.transpose(bank[:, t * P:(t + 1) * P], src[:, t, :], ident[:])
                last.then_inc(done, 1)

            pe.wait_ge(consts, 3)
            pe.wait_ge(w_in, 16)
            pe.wait_ge(msg_ready, 1)
            nc.tensor.matmul(aux_ps[:], w_sb[:, 1, :], msg[:], start=True, stop=True).then_inc(k_done, 1)
            for i, ((lo, hi), (t0, t1)) in enumerate(zip(Q_SLICES, TILE_SLICES)):
                pe.wait_ge(h_ready, i + 1)
                transposes(turn_ps[i], h_sb, h_turned, t0, t1)
                if i == 1:
                    for m in range(NT):
                        last = nc.tensor.matmul(turn_ps[0][:, m * D:(m + 1) * D], msg[:, m * P:(m + 1) * P],
                                                w_sb[:, 2, :], start=True, stop=True)
                    last.then_inc(v_done, 1)
                    pe.wait_ge(k_split, 1)
                pe.wait_ge(ht_ready, i + 1)
                nc.tensor.matmul((misc_ps, aux_ps)[i][:, 0:hi - lo], w_sb[:, 0, :], h_t[:, lo:hi],
                                 start=True, stop=True).then_inc(q_done[i], 1)

            def scores(u):
                t, h = divmod(u, HEADS)
                if u >= 2:
                    pe.wait_ge(masked, u - 1)
                if u == HEADS:
                    pe.wait_ge(q_stacked[1], 16 * len(Q_RUNS))
                nc.tensor.matmul(score_ps[u % 2], q_st[0:STACK, h, t * P:(t + 1) * P], k_st[0:STACK, h, :],
                                 start=True, stop=True).then_inc(scored, 1)

            def weighted_values(u):
                t, h = divmod(u, HEADS)
                pe.wait_ge(lo_moved, u + 1)
                if h == 0 and t >= 2:
                    pe.wait_ge(o_moved, t - 1)
                for i in range(2):
                    for m in range(NT):
                        last = nc.tensor.matmul(o_ps[t % 2][:, h * PARTS * DH:(h + 1) * PARTS * DH],
                                                prob_t[:, u % 2, i, m * P:(m + 1) * P],
                                                v_st[:, m, h].rearrange("p i c -> p (i c)"),
                                                start=(i == 0 and m == 0), stop=(i == 1 and m == NT - 1))
                last.then_inc(summed, 1)

            pe.wait_ge(k_stacked, 16 * len(K_RUNS))
            pe.wait_ge(q_stacked[0], 16 * len(Q_RUNS))
            scores(0)
            scores(1)
            for u in range(UNITS):
                if u + 2 < UNITS:
                    scores(u + 2)
                pe.wait_ge(exped, u + 1)
                if u >= 2:
                    pe.wait_ge(lo_moved, u - 1)
                if u == 0:
                    pe.wait_ge(v_split, 1)
                if u == 1:
                    pe.wait_ge(ht_ready, 2)
                for m in range(NT):
                    last = nc.tensor.transpose(turn_ps[u % 2][:, m * P:(m + 1) * P],
                                               prob[:, u % RING, m * P:(m + 1) * P], ident[:])
                last.then_inc(turned, 1)
                if u == LAG:
                    pe.wait_ge(v_split, 2 * PARTS)
                if u >= LAG:
                    weighted_values(u - LAG)
            for u in range(UNITS - LAG, UNITS):
                weighted_values(u)

            for i, (t0, t1) in enumerate(GROUPS):
                pe.wait_ge(o_ready, i + 1)
                transposes(turn_ps[i], o_sb, o_turned, t0, t1)
            for i, (t0, t1) in enumerate(GROUPS):
                pe.wait_ge(ot_ready, i + 1)
                for t in range(t0, t1):
                    last = nc.tensor.matmul((misc_ps, aux_ps)[i][:, t * D:(t + 1) * D], o_t[:, t * P:(t + 1) * P],
                                            w_sb[:, 3, :], start=True, stop=True)
                last.then_inc(projected, 1)
            for i, (t0, t1) in enumerate(GROUPS):
                pe.wait_ge(h_ready, 3 + i)
                transposes(turn_ps[i], h_sb, h_turned, t0, t1)
            pe.wait_ge(w1_in, 16)
            for i, (t0, t1) in enumerate(GROUPS):
                pe.wait_ge(ht_ready, 3 + i)
                for t in range(t0, t1):
                    last = nc.tensor.matmul(s_ps[:, i, (t - t0) * NODES_PAD:(t - t0) * NODES_PAD + NODES],
                                            h_t[:, t * P:(t + 1) * P], w1_sb[:], start=True, stop=True)
                last.then_inc(node_scored, 1)

            pe.wait_ge(consts2, 10)
            pe.wait_ge(path_ready, 1)
            for t in range(TILES):
                last = nc.tensor.matmul(aux_ps[:, 0:1], path[:, t, LEAF0:NODES], ones_h[:, 0:1],
                                        start=(t == 0), stop=(t == TILES - 1))
            last.then_inc(leaves_counted, 1)
            pe.wait_ge(leaf_count_ready, 1)
            for t in range(TILES):
                dst = turn_ps[0][:, t * LEAVES:(t + 1) * LEAVES]
                nc.tensor.matmul(dst, leaf_count[:], before[:], start=True, stop=False)
                for other in range(t):
                    nc.tensor.matmul(dst, ones_h[:], path[:, other, LEAF0:NODES], start=False, stop=False)
                last = nc.tensor.matmul(dst, before[:], path[:, t, LEAF0:NODES], start=False, stop=True)
            last.then_inc(placed, 1)

            def by_order(dst, s, values, stop=True):
                n = len(values(0))
                for t in range(TILES):
                    for i, value in enumerate(values(t)):
                        last = nc.tensor.matmul(dst, perm[:, t, s * P:(s + 1) * P], value,
                                                start=(t == 0 and i == 0), stop=(t == TILES - 1 and i == n - 1))
                return last

            pe.wait_ge(pos_ready, 1)
            for c in range(2):
                for t in range(TILES):
                    last = nc.tensor.matmul(aux_ps[:, c * (TILES + 1):(c + 1) * (TILES + 1)],
                                            path[:, t, c * P:(c + 1) * P], from_tile[:, t, :],
                                            start=(t == 0), stop=(t == TILES - 1))
            last.then_inc(counted, 1)
            pe.wait_ge(active_ready, 1)
            nc.tensor.matmul(misc_ps[:, 0:TILES], before[:], active_h[:, 0, :], start=True, stop=True)
            nc.tensor.matmul(misc_ps[:, TILES:2 * TILES], ones_h[:], active_h[:, 0, :], start=True, stop=False)
            nc.tensor.matmul(misc_ps[:, TILES:2 * TILES], before[:], active_h[:, 1, :], start=False, stop=True)
            for c in range(2):
                last = nc.tensor.matmul(misc_ps[0:1, 2 * TILES:3 * TILES], ones_h[:, 0:1], active_h[:, c, :],
                                        start=(c == 0), stop=(c == 1))
            last.then_inc(ranked, 1)

            pe.wait_ge(perm_ready, 1)
            for s in range(TILES):
                last = by_order(turn_ps[0][:, s:s + 1], s, lambda t: [token_col[:, t:t + 1]])
            last.then_inc(tokens_sorted, 1)
            for s in range(TILES):
                last = by_order(s_ps[:, 2 + s // 2, (s % 2) * NODES_PAD:(s % 2 + 1) * NODES_PAD], s,
                                lambda t: [path[:, t, :]])
            last.then_inc(path_sorted, 1)
            pe.wait_ge(chosen_ready, 1)
            for half in range(2):
                for c in range(2):
                    last = nc.tensor.matmul(s_ps[0:1, half, :], node_col[:, c:c + 1],
                                            chosen[:, c, half * 512:(half + 1) * 512],
                                            start=(c == 0), stop=(c == 1))
            last.then_inc(listed, 1)
            pe.wait_ge(picked_split, 2 * PARTS - 1)
            pe.wait_ge(counts_moved, 1)
            for s in range(TILES):
                last = by_order(aux_ps[:, s * PARTS * LEVELS:(s + 1) * PARTS * LEVELS], s,
                                lambda t: [picked_p[:, t].rearrange("p i l -> p (i l)")])
            last.then_inc(weight_sorted, 1)
            pe.wait_ge(h_split, 2)
            for t in range(TILES):
                for i in range(2):
                    last = nc.tensor.matmul(turn_ps[1][:], h_p[:, t, i, :], perm[:, t, :],
                                            start=(t == 0 and i == 0), stop=(t == TILES - 1 and i == 1))
            last.then_inc(h_sorted, 1)
            for i in range(W2_PARTS):
                pe.wait_ge(w2_in[i], 16)
            pe.wait_ge(b2_in, 32)
            pe.wait_ge(lists_ready, 2)
            lengths = list_lengths(nc, pe.engine, entries)
            pe.wait_ge(tokens_moved, 1)
            pe.wait_ge(hs_ready, 1)
            pe.wait_ge(coef_ready, 1)
            for c in range(2):
                transposes((turn_ps[1], misc_ps)[c], coef[:, :, c * P:(c + 1) * P], coef_turned)

            def products(s, found, e):
                for half in range(2):
                    pe.wait_ge(added[half], e)
                    if (s, half) == (0, 1):
                        pe.wait_ge(coef_t_ready, 2)
                    if half == 1 and 1 <= s <= len(GROUPS):
                        pe.wait_ge(bias_moved, s)
                    for j in range(HALF):
                        if j == BY_DVE[half]:
                            ins.then_inc(multiplied[half], STEP)
                            pe.wait_ge(scaled[half], e)
                        ins = nc.tensor.matmul(product_ps[half][j], hs_t[:, s * P:(s + 1) * P],
                                               w2[:, bass.ds(found[HALF * half + j], 1), :
                                                  ].rearrange("p n o -> p (n o)"), start=True, stop=True)
                    ins.then_inc(multiplied_last[half], STEP)

            def biases(s, end):
                if s < len(GROUPS):
                    pe.wait_ge(scaled[1], end)
                    for tile in range(*GROUPS[s]):
                        for c in range(2):
                            last = nc.tensor.matmul(misc_ps[:, tile * D:(tile + 1) * D],
                                                    coef_t[:, c, tile * P:(tile + 1) * P], b2_sb[:, c, :],
                                                    start=(c == 0), stop=(c == 1))
                    last.then_inc(biased, 1)

            tile_turns(nc, pe, lengths, nodes, products, biases)

        @block.vector
        def _(dve):
            steps = [0]

            def then(ins):
                steps[0] += 1
                ins.then_inc(vstep, 1)
                dve.wait_ge(vstep, steps[0])

            def statistics(src, t0=0, t1=TILES):
                for t in range(t0, t1):
                    ins = nc.vector.bn_stats(stats[:, t, :], src[:, t, :])
                then(ins)
                for t in range(t0, t1):
                    ins = nc.vector.bn_aggr(mv[:, t, :], stats[:, t, :])
                then(ins)
                nc.vector.tensor_scalar(veps[:, t0:t1], mv[:, t0:t1, 1], EPS, None, ALU.add).then_inc(veps_ready, 1)

            def normalise(src, nth, t0=0, t1=TILES):
                dve.wait_ge(rstd_ready, nth)
                for t in range(t0, t1):
                    ins = nc.vector.tensor_scalar(h_sb[:, t, :], src[:, t, :], mv[:, t, 0:1],
                                                  rstd[:, t:t + 1], ALU.subtract, ALU.mult)
                ins.then_inc(h_ready, 1)

            def split(src, parts, done, at=0):
                for i in range(len(parts)):
                    nc.vector.tensor_copy(parts[i], src).then_inc(done, 1)
                    at += 1
                    if i < len(parts) - 1:
                        dve.wait_ge(done, at)
                        nc.vector.tensor_tensor(src, src, parts[i], ALU.subtract).then_inc(done, 1)
                        at += 1
                        dve.wait_ge(done, at)

            for half in range(2):
                dve.sem_inc(added[half], STEP)
            dve.wait_ge(neigh_in, 16)
            dve.wait_ge(col_in, 16)
            nc.vector.tensor_scalar(msg[:], msg[:], col_sb[:, 3:4], None, ALU.add).then_inc(msg_ready, 1)
            dve.wait_ge(x_in, 16)
            for t0, t1 in TILE_SLICES:
                statistics(x_sb, t0, t1)

            def turn_back(i):
                lo, hi = Q_SLICES[i]
                dve.wait_ge(h_turned, i + 1)
                nc.vector.tensor_copy(h_t[:, lo:hi], turn_ps[i][:, lo:hi]).then_inc(ht_ready, 1)

            def key_rest(i):
                dve.wait_ge(k_split, 2 * i + 2)
                nc.vector.tensor_tensor(k_f, k_f, k_p[:, i, :], ALU.subtract).then_inc(k_split, 1)

            def query_parts(i):
                lo, hi = Q_SLICES[i]
                dve.wait_ge(q_done[i], 1)
                nc.vector.tensor_scalar(q_f[:, lo:hi], (misc_ps, aux_ps)[i][:, 0:hi - lo], col_sb[:, 0:1], -SCALE,
                                        ALU.add, ALU.mult).then_inc(q_split[i], 1)
                dve.wait_ge(q_split[i], 1)
                split(q_f[:, lo:hi], [q_p[:, j, lo:hi] for j in range(PARTS)], q_split[i], 1)

            normalise(x_sb, 1, *TILE_SLICES[0])
            key_rest(0)
            turn_back(0)
            normalise(x_sb, 2, *TILE_SLICES[1])
            key_rest(1)
            query_parts(0)
            turn_back(1)
            dve.wait_ge(v_done, 1)
            dve.wait_ge(row_in, 16)
            nc.vector.tensor_tensor(v_f.rearrange("p (m d) -> p m d", d=D),
                                    turn_ps[0][:].rearrange("p (m d) -> p m d", d=D),
                                    row_sb[:, BV:BV + D].unsqueeze(1).to_broadcast([P, NT, D]), ALU.add
                                    ).then_inc(v_split, 1)
            query_parts(1)
            dve.wait_ge(adj_in, 16)
            nc.vector.tensor_scalar(mask[:], adj_sb, 0.0, MASKED, ALU.is_equal, ALU.mult).then_inc(mask_ready, 1)
            dve.wait_ge(mask_ready, 1)
            for u in range(UNITS + LAG):
                if u < UNITS:
                    t, h = divmod(u, HEADS)
                    dve.wait_ge(scored, u + 1)
                    if u >= RING:
                        dve.wait_ge(turned, u - RING + 1)
                    nc.vector.tensor_tensor_reduce(out=prob[:, u % RING, :], in0=score_ps[u % 2],
                                                   in1=mask[:, t, :], scale=1.0, scalar=3.0e38,
                                                   op0=ALU.add, op1=ALU.min,
                                                   accum_out=negmax[:, t, h:h + 1]).then_inc(masked, 1)
                if u >= LAG:
                    v = u - LAG
                    dve.wait_ge(hi_moved, v + 1)
                    nc.vector.tensor_tensor(prob_t[:, v % 2, 1, :], turn_ps[v % 2][:], prob_t[:, v % 2, 0, :],
                                            ALU.subtract).then_inc(lo_moved, 1)
                if u >= HEADS + LAG + 1 and (u - LAG - 1) % HEADS == 0 or u == UNITS + LAG - 1:
                    t = (u - LAG - 1) // HEADS - 1 if u < UNITS + LAG - 1 else TILES - 1
                    dve.wait_ge(summed, HEADS * (t + 1))
                    nc.vector.tensor_reduce(o_sb[:, t, :].rearrange("p (h c) -> p h c", c=DH),
                                            o_ps[t % 2].rearrange("p (h i c) -> p h c i", i=PARTS, c=DH),
                                            AX_X, ALU.add).then_inc(o_moved, 1)

            dve.wait_ge(exped, UNITS)
            dve.wait_ge(masked, UNITS)
            nc.vector.reciprocal(psums[:], psums[:]).then_inc(live_ready, 1)
            nc.vector.tensor_scalar(live[:], negmax[:], 0.5 * MASKED, None, ALU.is_lt).then_inc(live_ready, 1)
            dve.wait_ge(live_ready, 2)
            then(nc.vector.tensor_tensor(live[:], live[:], psums[:], ALU.mult))
            dve.wait_ge(o_moved, TILES)
            by_head = o_sb[:].rearrange("p t (h c) -> p (t h) c", c=DH)
            scale = live[:].rearrange("p t h -> p (t h)").unsqueeze(2)
            for t0, t1 in GROUPS:
                part = by_head[:, t0 * HEADS:t1 * HEADS, :]
                nc.vector.tensor_tensor(part, part, scale[:, t0 * HEADS:t1 * HEADS, :].to_broadcast(
                    [P, (t1 - t0) * HEADS, DH]), ALU.mult).then_inc(o_ready, 1)
            dve.wait_ge(x_biased, 1)
            for i, (t0, t1) in enumerate(GROUPS):
                dve.wait_ge(projected, i + 1)
                nc.vector.tensor_tensor(x1[:, t0:t1], x_sb[:, t0:t1], (misc_ps, aux_ps)[i][:, t0 * D:t1 * D
                                        ].rearrange("p (t d) -> p t d", d=D), ALU.add).then_inc(x1_ready, 1)
                dve.wait_ge(x1_ready, i + 1)
                statistics(x1, t0, t1)
            for i, (t0, t1) in enumerate(GROUPS):
                normalise(x1, 3 + i, t0, t1)
            dve.wait_ge(h_ready, 4)
            nc.vector.tensor_copy(h_p[:, :, 0, :], h_sb[:]).then_inc(h_split, 1)
            dve.wait_ge(h_split, 1)
            nc.vector.tensor_tensor(h_p[:, :, 1, :], h_sb[:], h_p[:, :, 0, :], ALU.subtract).then_inc(h_split, 1)
            node_scores = s_ps[:, 0:2, :].rearrange("p b (t n) -> p (b t) n", n=NODES_PAD)
            b1 = row_sb[:, B1:].unsqueeze(1)
            dve.wait_ge(consts2, 10)
            for i, (t0, t1) in enumerate(GROUPS):
                dve.wait_ge(node_scored, i + 1)
                then(nc.vector.tensor_tensor(scores_b[:, t0:t1, 0:LEAF0], node_scores[:, t0:t1, 0:LEAF0],
                                             b1[:, :, 0:LEAF0].to_broadcast([P, t1 - t0, LEAF0]), ALU.add))
                nc.vector.tensor_scalar(sides[:, t0:t1, 0:LEAF0, 0], scores_b[:, t0:t1, 0:LEAF0], 0.0, None,
                                        ALU.is_le)
                ins = nc.vector.tensor_scalar(sides[:, t0:t1, 0:LEAF0, 1], scores_b[:, t0:t1, 0:LEAF0], 0.0, None,
                                              ALU.is_gt)
            then(ins)
            for l in range(DEPTH):
                n, at = 2 ** l, 2 ** l - 1
                child = path[:, :, 2 * at + 1:2 * at + 1 + 2 * n].rearrange("p t (n c) -> p t n c", c=2)
                ins = nc.vector.tensor_tensor(child, sides[:, :, at:at + n, :], path[:, :, at:at + n].unsqueeze(3
                                              ).to_broadcast([P, TILES, n, 2]), ALU.mult)
                if l < DEPTH - 1:
                    then(ins)
            ins.then_inc(path_ready, 1)
            dve.wait_ge(leaves_counted, 1)
            nc.vector.tensor_copy(leaf_count[:], aux_ps[:, 0:1].to_broadcast([P, P])).then_inc(leaf_count_ready, 1)
            then(nc.vector.tensor_tensor(scores_b[:, :, LEAF0:NODES], node_scores[:, :, LEAF0:NODES],
                                         b1[:, :, LEAF0:NODES].to_broadcast([P, TILES, LEAVES]), ALU.add))
            dve.wait_ge(path_ready, 1)
            then(nc.vector.tensor_tensor(prod[:, :, 0:NODES], scores_b[:, :, 0:NODES], path[:, :, 0:NODES],
                                         ALU.mult))
            dve.wait_ge(placed, 1)
            then(nc.vector.tensor_tensor(place_l, turn_ps[0][:].rearrange("p (t n) -> p t n", n=LEAVES),
                                         path[:, :, LEAF0:NODES], ALU.mult))
            then(nc.vector.tensor_reduce(pos[:], place_l, AX_X, ALU.add))
            nc.vector.tensor_tensor(from_tile[:], pos[:].unsqueeze(2).to_broadcast([P, TILES, TILES + 1]),
                                    tile_row[:].unsqueeze(1).to_broadcast([P, TILES, TILES + 1]), ALU.is_ge
                                    ).then_inc(pos_ready, 1)
            for t in range(TILES):
                ins = nc.vector.tensor_scalar(perm[:, t, :], count_row[:], pos[:, t:t + 1], None, ALU.is_equal)
            ins.then_inc(perm_ready, 1)
            dve.wait_ge(counted, 1)
            counts = aux_ps[:, 0:2 * (TILES + 1)].rearrange("p (c t) -> p c t", c=2)
            nc.vector.tensor_copy(counts_sb[:], counts).then_inc(counts_moved, 1)
            dve.wait_ge(counts_moved, 1)
            nc.vector.tensor_tensor(active_h[:], counts_sb[:, :, 0:TILES], counts_sb[:, :, 1:], ALU.is_gt
                                    ).then_inc(active_ready, 1)
            then(nc.vector.tensor_tensor(active[:].rearrange("p (c t) -> p c t", c=2), counts_sb[:, :, 0:TILES],
                                         counts_sb[:, :, 1:], ALU.is_gt))
            for l in range(LEVELS):
                ins = nc.vector.tensor_reduce(picked[:, :, l], prod[:, :, 2 ** l - 1:2 ** (l + 1) - 1], AX_X, ALU.add)
            ins.then_inc(picked_ready, 1)
            dve.wait_ge(tokens_sorted, 1)
            nc.vector.tensor_copy(token_s[:], turn_ps[0][:, 0:TILES]).then_inc(tokens_moved, 1)
            dve.wait_ge(ranked, 1)
            then(nc.vector.tensor_copy(rank[:], misc_ps[:, 0:2 * TILES]))
            for c in range(2):
                for s in range(TILES):
                    i = c * TILES + s
                    ins = nc.vector.tensor_scalar(chosen[:, c, s * NODES_PAD:(s + 1) * NODES_PAD],
                                                  count_row[:, 0:NODES_PAD], rank[:, i:i + 1],
                                                  active[:, i:i + 1], ALU.is_equal, ALU.mult)
            ins.then_inc(chosen_ready, 1)
            length = misc_ps[0:1, 2 * TILES:3 * TILES]
            then(nc.vector.tensor_scalar(turned_up[:], length, STEP - 1.0, None, ALU.add))
            nc.vector.tensor_scalar(entries[:], turned_up[:], -STEP, None, ALU.bitwise_and).then_inc(lists_ready, 1)
            dve.wait_ge(weighted, 2)
            split(picked[:], [picked_p[:, :, i, :] for i in range(PARTS)], picked_split)
            dve.wait_ge(weight_sorted, 1)
            parts = aux_ps[:, 0:TILES * PARTS * LEVELS].rearrange("p (s i l) -> p s l i", i=PARTS, l=LEVELS)
            then(nc.vector.tensor_reduce(weight_s[:], parts, AX_X, ALU.add))
            dve.wait_ge(path_s_ready, 1)
            for l in range(LEVELS):
                n = 2 ** l
                nc.vector.tensor_tensor(coef[:, :, n - 1:2 * n - 1], path_s[:, :, n - 1:2 * n - 1],
                                        weight_s[:, :, l:l + 1].to_broadcast([P, TILES, n]), ALU.mult)
            nc.vector.memset(coef[:, :, NODES:NODES_PAD], 0.0).then_inc(coef_ready, 1)
            dve.wait_ge(x1_sorted, 16 * TILES)
            dve.wait_ge(acc_zero, 1)
            dve.wait_ge(lists_ready, 2)
            lengths = list_lengths(nc, dve.engine, entries)

            def add_up(s, found, e):
                for half in range(2):
                    dve.wait_ge(multiplied[half], e)
                    dve.wait_ge(added[half], e)
                    for j in range(BY_DVE[half]):
                        mine = acc[:, half * HALF + j, s, :]
                        ins = nc.vector.scalar_tensor_tensor(
                            out=mine, in0=product_ps[half][j], scalar=coef[:, s, bass.ds(found[HALF * half + j], 1)],
                            in1=mine, op0=ALU.mult, op1=ALU.add)
                    ins.then_inc(added[half], STEP)

            def sum_up(s, end):
                if not SUMMED_AFTER[s]:
                    return
                for half in range(2):
                    dve.wait_ge(added[half], end)
                    dve.wait_ge(pooled[half], end)
                dve.wait_ge(bias_moved, min(s, len(GROUPS)))
                for tile in SUMMED_AFTER[s]:
                    nc.vector.tensor_reduce(result[:, tile, :], acc[:, :, tile, :].rearrange("p j d -> p d j"),
                                            AX_X, ALU.add).then_inc(tile_done, 1)

            tile_turns(nc, dve, lengths, nodes, add_up, sum_up)


_INS = ("x", "adj", "neigh_t", "w_t", "cols", "rows", "w1_t", "w2_t", "b2")


def kernel(**inputs):
    import numpy as np
    import concourse.bacc as bacc
    from concourse.bass_utils import run_bass_kernel_spmd as run

    g = {k: np.asarray(v) for k, v in inputs.items()}
    by_channel = np.arange(D).reshape(HEADS, DH).T.reshape(-1)
    wq, wk = g["L0_gnn_Wq"][by_channel], g["L0_gnn_Wk"][by_channel]
    bq, bk = g["L0_gnn_bq"][by_channel], g["L0_gnn_bk"][by_channel]
    laid = {
        "x": g["x"],
        "adj": g["adj"],
        "neigh_t": g["L0_gnn_h_neigh"].T,
        "w_t": np.concatenate([wq.T, wk.T, g["L0_gnn_Wv"].T, g["L0_gnn_Wo"].T], axis=1),
        "cols": np.stack([bq, bk, g["L0_gnn_E"][0], g["L0_gnn_E"][1]], axis=1),
        "rows": np.concatenate([g["L0_gnn_bv"], g["L0_gnn_bo"], g["L0_ffn_b1s"]])[None],
        "w1_t": g["L0_ffn_w1s"].T,
        "w2_t": g["L0_ffn_w2s"].transpose(1, 0, 2).reshape(D, NODES * D),
        "b2": g["L0_ffn_b2s"],
    }
    nc = bacc.Bacc("TRN2", target_bir_lowering=False, num_devices=1)
    arrays, args = {}, []
    for name in _INS:
        a = np.ascontiguousarray(laid[name])
        arrays[f"in_{name}"] = a
        args.append(nc.dram_tensor(f"in_{name}", a.shape, mybir.dt.from_np(a.dtype), kind="ExternalInput").ap())
    for name in ("k_parts", "q_parts"):
        args.append(nc.dram_tensor(name, (PARTS, D, 512), BF16, kind="Internal").ap())
    args.append(nc.dram_tensor("x1_rows", (N_TOK, D), F32, kind="Internal").ap())
    args.append(nc.dram_tensor("out_x", (N_TOK, D), F32, kind="ExternalOutput").ap())
    gnn_ffn_kernel(nc, *args)
    result = run(nc, [arrays], core_ids=[0])
    return result.results[0]["out_x"]
```
